# Optimizing a Trainium2 kernel written in Bass

```python
import numpy as np
import jax
import jax.numpy as jnp

def _softmax(x, axis=-1):
    return jax.nn.softmax(x, axis=axis)

def _gelu(x):
    return jax.nn.gelu(x, approximate=True)

def _silu(x):
    return jax.nn.silu(x)

def _sigmoid(x):
    return jax.nn.sigmoid(x)

def _layernorm(x, axis=-1, eps=1e-05):
    m = jnp.mean(x, axis=axis, keepdims=True)
    v = jnp.var(x, axis=axis, keepdims=True)
    return (x - m) / jnp.sqrt(v + eps)

def _scatter_add(tgt, idx, src, axis=0):
    return tgt.at[idx].add(src)

def _segment_sum(src, seg, n):
    return jax.ops.segment_sum(src, seg, n)
kernel_name = 'mk_gnn_resnorm_d2_gnn_r32_51dab5'

def setup_inputs(seed: int=0):
    np.random.seed(seed)
    _w = jnp.asarray

    def _rec_inputs():
        import jax
        import jax.numpy as jnp
        _gk = jax.random.key(seed)
        x = -0.0005963 + 1.001 * jax.random.normal(jax.random.fold_in(_gk, 1), (96, 1024), jnp.float32)
        src = jax.random.randint(jax.random.fold_in(_gk, 2), (3072,), 0, 96, jnp.int32)
        dst = jax.random.randint(jax.random.fold_in(_gk, 3), (3072,), 0, 96, jnp.int32)
        _o = jnp.argsort(dst, stable=True)
        src = src[_o]
        dst = dst[_o]
        edge_type_5 = jax.random.randint(jax.random.fold_in(_gk, 12), (3072,), 0, 5, jnp.int32)
        edge_type_8 = jax.random.randint(jax.random.fold_in(_gk, 13), (3072,), 0, 8, jnp.int32)
        return (x, src, dst, edge_type_5, edge_type_8)
    x, src, dst, edge_type_5, edge_type_8 = _rec_inputs()

    def _L0_gnn_setup():
        import jax, jax.numpy as jnp
        import numpy as np
        N = 96
        E = 3072
        IN_F = 1024
        OUT_F = 1024
        H = 16
        D = OUT_F // H
        NUM_ETYPES = 4

        def _build_mask(edge_index, edge_type, edge_type_weights, dtype):
            src, dst = (edge_index[0], edge_index[1])
            w = jax.nn.softplus(edge_type_weights)
            mask = jnp.full((N, N), -jnp.inf, dtype=dtype)
            mask = mask.at[src, dst].set(w[edge_type - 1])
            diag = jnp.diagonal(mask)
            idx = jnp.arange(N)
            mask = mask.at[idx, idx].set(jnp.where(jnp.isneginf(diag), w[3], diag))
            return mask
        key = jax.random.key(seed)
        ks = jax.random.split(key, 20)
        p = lambda k, shape: jax.random.normal(k, shape, dtype=jnp.float32) * 0.02
        return {'x': jax.random.normal(ks[0], (N, IN_F), dtype=jnp.float32), 'edge_index': jax.random.randint(ks[1], (2, E), 0, N), 'edge_type': jax.random.randint(ks[2], (E,), 1, NUM_ETYPES + 1), 'edge_type_weights': jnp.ones((NUM_ETYPES,), jnp.float32) + 0.1 * jax.random.normal(ks[3], (NUM_ETYPES,), dtype=jnp.float32), 'wq': p(ks[4], (OUT_F, IN_F)), 'bq': p(ks[5], (OUT_F,)), 'wk': p(ks[6], (OUT_F, IN_F)), 'bk': p(ks[7], (OUT_F,)), 'wv': p(ks[8], (OUT_F, IN_F)), 'bv': p(ks[9], (OUT_F,)), 'wiq': p(ks[10], (OUT_F, OUT_F)), 'biq': p(ks[11], (OUT_F,)), 'wik': p(ks[12], (OUT_F, OUT_F)), 'bik': p(ks[13], (OUT_F,)), 'wiv': p(ks[14], (OUT_F, OUT_F)), 'biv': p(ks[15], (OUT_F,)), 'wo': p(ks[16], (OUT_F, OUT_F)), 'bo': p(ks[17], (OUT_F,))}
    _L0_gnn_all = _L0_gnn_setup()
    _L0_gnn_in = {k: v for k, v in _L0_gnn_all.items() if k in ('edge_type_weights', 'wq', 'bq', 'wk', 'bk', 'wv', 'bv', 'wiq', 'biq', 'wik', 'bik', 'wiv', 'biv', 'wo', 'bo')}
    del _L0_gnn_all

    def _L1_gnn_setup():
        import jax, jax.numpy as jnp
        import numpy as np
        N, D, R, E = (10000, 1024, 8, 2500)

        def _rgcn(x, edge_index, edge_type, weight, root, bias):
            src, dst = (edge_index[0], edge_index[1])
            msgs = x[src]
            out = x @ root + bias
            n = x.shape[0]
            for r in range(weight.shape[0]):
                mask = (edge_type == r).astype(x.dtype)
                sums = jax.ops.segment_sum(msgs * mask[:, None], dst, num_segments=n)
                cnt = jax.ops.segment_sum(mask, dst, num_segments=n)
                mean = sums / jnp.maximum(cnt, 1.0)[:, None]
                out = out + mean @ weight[r]
            return out
        key = jax.random.key(seed)
        ks = jax.random.split(key, 8)
        s = 1.0 / np.sqrt(D)
        x = jax.random.normal(ks[0], (N, D), dtype=jnp.float32)
        edge_index = jax.random.randint(ks[1], (2, E), 0, N, dtype=jnp.int64)
        edge_type = jax.random.randint(ks[2], (E,), 0, R, dtype=jnp.int64)
        weight = jax.random.normal(ks[3], (R, D, D), dtype=jnp.float32) * s
        root = jax.random.normal(ks[4], (D, D), dtype=jnp.float32) * s
        bias = jnp.zeros((D,), dtype=jnp.float32)
        w_gate = jax.random.normal(ks[5], (2 * D, D), dtype=jnp.float32) * (1.0 / np.sqrt(2 * D))
        b_gate = jnp.zeros((D,), dtype=jnp.float32)
        return {'x': x, 'edge_index': edge_index, 'edge_type': edge_type, 'weight': weight, 'root': root, 'bias': bias, 'w_gate': w_gate, 'b_gate': b_gate}
    _L1_gnn_all = _L1_gnn_setup()
    _L1_gnn_in = {k: v for k, v in _L1_gnn_all.items() if k in ('weight', 'root', 'bias', 'w_gate', 'b_gate')}
    del _L1_gnn_all
    return {'x': x, 'src': src, 'dst': dst, 'edge_type_5': edge_type_5, 'edge_type_8': edge_type_8, 'L0_gnn_edge_type_weights': _L0_gnn_in['edge_type_weights'], 'L0_gnn_wq': _L0_gnn_in['wq'], 'L0_gnn_bq': _L0_gnn_in['bq'], 'L0_gnn_wk': _L0_gnn_in['wk'], 'L0_gnn_bk': _L0_gnn_in['bk'], 'L0_gnn_wv': _L0_gnn_in['wv'], 'L0_gnn_bv': _L0_gnn_in['bv'], 'L0_gnn_wiq': _L0_gnn_in['wiq'], 'L0_gnn_biq': _L0_gnn_in['biq'], 'L0_gnn_wik': _L0_gnn_in['wik'], 'L0_gnn_bik': _L0_gnn_in['bik'], 'L0_gnn_wiv': _L0_gnn_in['wiv'], 'L0_gnn_biv': _L0_gnn_in['biv'], 'L0_gnn_wo': _L0_gnn_in['wo'], 'L0_gnn_bo': _L0_gnn_in['bo'], 'L1_gnn_weight': _L1_gnn_in['weight'], 'L1_gnn_root': _L1_gnn_in['root'], 'L1_gnn_bias': _L1_gnn_in['bias'], 'L1_gnn_w_gate': _L1_gnn_in['w_gate'], 'L1_gnn_b_gate': _L1_gnn_in['b_gate']}

def reference(x, src, dst, edge_type_5, edge_type_8, L0_gnn_edge_type_weights, L0_gnn_wq, L0_gnn_bq, L0_gnn_wk, L0_gnn_bk, L0_gnn_wv, L0_gnn_bv, L0_gnn_wiq, L0_gnn_biq, L0_gnn_wik, L0_gnn_bik, L0_gnn_wiv, L0_gnn_biv, L0_gnn_wo, L0_gnn_bo, L1_gnn_weight, L1_gnn_root, L1_gnn_bias, L1_gnn_w_gate, L1_gnn_b_gate):
    import jax
    import jax.numpy as jnp

    def _L0_gnn_ref(x, edge_index, edge_type, edge_type_weights, wq, bq, wk, bk, wv, bv, wiq, biq, wik, bik, wiv, biv, wo, bo):
        import jax, jax.numpy as jnp
        import numpy as np
        N = 96
        E = 3072
        IN_F = 1024
        OUT_F = 1024
        H = 16
        D = OUT_F // H
        NUM_ETYPES = 4

        def _build_mask(edge_index, edge_type, edge_type_weights, dtype):
            src, dst = (edge_index[0], edge_index[1])
            w = jax.nn.softplus(edge_type_weights)
            mask = jnp.full((N, N), -jnp.inf, dtype=dtype)
            mask = mask.at[src, dst].set(w[edge_type - 1])
            diag = jnp.diagonal(mask)
            idx = jnp.arange(N)
            mask = mask.at[idx, idx].set(jnp.where(jnp.isneginf(diag), w[3], diag))
            return mask
        q = x @ wq.T + bq
        k = x @ wk.T + bk
        v = x @ wv.T + bv
        q2 = (q @ wiq.T + biq).reshape(N, H, D).transpose(1, 0, 2)
        k2 = (k @ wik.T + bik).reshape(N, H, D).transpose(1, 0, 2)
        v2 = (v @ wiv.T + biv).reshape(N, H, D).transpose(1, 0, 2)
        mask = _build_mask(edge_index, edge_type, edge_type_weights, x.dtype)
        scale = 1.0 / np.sqrt(D).astype(np.float32)
        scores = jnp.einsum('hnd,hmd->hnm', q2, k2) * scale + mask[None]
        attn = jax.nn.softmax(scores, axis=-1)
        out = jnp.einsum('hnm,hmd->hnd', attn, v2)
        out = out.transpose(1, 0, 2).reshape(N, OUT_F)
        return out @ wo.T + bo

    def _L1_gnn_ref(x, edge_index, edge_type, weight, root, bias, w_gate, b_gate):
        import jax, jax.numpy as jnp
        import numpy as np
        N, D, R, E = (10000, 1024, 8, 2500)

        def _rgcn(x, edge_index, edge_type, weight, root, bias):
            src, dst = (edge_index[0], edge_index[1])
            msgs = x[src]
            out = x @ root + bias
            n = x.shape[0]
            for r in range(weight.shape[0]):
                mask = (edge_type == r).astype(x.dtype)
                sums = jax.ops.segment_sum(msgs * mask[:, None], dst, num_segments=n)
                cnt = jax.ops.segment_sum(mask, dst, num_segments=n)
                mean = sums / jnp.maximum(cnt, 1.0)[:, None]
                out = out + mean @ weight[r]
            return out
        u = _rgcn(x, edge_index, edge_type, weight, root, bias)
        z = jnp.concatenate([u, x], axis=1) @ w_gate + b_gate
        h = jnp.tanh(u) * z + x * (1.0 - z)
        return h
    edge_index = jnp.stack([src, dst])
    x = _layernorm(x + _L0_gnn_ref(x, edge_index, edge_type_5, L0_gnn_edge_type_weights, L0_gnn_wq, L0_gnn_bq, L0_gnn_wk, L0_gnn_bk, L0_gnn_wv, L0_gnn_bv, L0_gnn_wiq, L0_gnn_biq, L0_gnn_wik, L0_gnn_bik, L0_gnn_wiv, L0_gnn_biv, L0_gnn_wo, L0_gnn_bo), axis=-1)
    x = _layernorm(x + _L1_gnn_ref(x, edge_index, edge_type_8, L1_gnn_weight, L1_gnn_root, L1_gnn_bias, L1_gnn_w_gate, L1_gnn_b_gate), axis=-1)
    return x

_drawn_inputs = setup_inputs


def setup_inputs(seed=0):
    import zlib

    import numpy as np

    out = dict(_drawn_inputs(seed))
    spreads = {'L1_gnn_bias': (0.0, 0.1), 'L1_gnn_b_gate': (0.0, 0.1)}
    factors = {'L0_gnn_edge_type_weights': 24.537,
     'L0_gnn_wq': 5.376,
     'L0_gnn_bq': 8.0,
     'L0_gnn_wk': 5.38,
     'L0_gnn_bk': 64.0,
     'L0_gnn_bv': 4.567,
     'L0_gnn_wiq': 5.406,
     'L0_gnn_biq': 8.0,
     'L0_gnn_wik': 5.374,
     'L0_gnn_bik': 64.0,
     'L0_gnn_biv': 2.788}
    for name, (base, spread) in spreads.items():
        noise = np.random.default_rng([zlib.crc32(name.encode()), seed]).standard_normal(out[name].shape)
        drawn = base * np.exp(spread * noise) if base else spread * noise
        out[name] = jnp.asarray(drawn.astype(out[name].dtype))
    for name, factor in factors.items():
        out[name] = (out[name] * factor).astype(out[name].dtype)
    return out
```

```python
from contextlib import ExitStack

import concourse.bass as bass
from concourse import mybir

NODES = 96
EDGES = 3072
FEATURES = 1024
HEADS = 16
HEAD_DIM = FEATURES // HEADS
RELATIONS = 8
CLASSES = 4
P = 128
CHUNKS = FEATURES // P
BANK = 512
HALVES = FEATURES // BANK
QUARTERS = 4
CHUNKS_PER_QUARTER = CHUNKS // QUARTERS
QUARTER = CHUNKS_PER_QUARTER * FEATURES
MATRICES = 18
RAW_SLOTS = 2 * QUARTERS
SPLIT_SLOTS = 4
SPLITS = (QUARTERS - 1) * CHUNKS_PER_QUARTER
EDGE_CHUNKS = EDGES // P
SPAN = CHUNKS * NODES
ROOT, REL0, GATE_U = 8, 9, 17
HEADS_PER_GROUP = 4
GROUPS = HEADS // HEADS_PER_GROUP
NO_EDGE = -1.0e30
PACK = 4096.0
BIG_KEY = 16384.0
ROUND = 12582912.0
EPS = 1e-5


def gnn_block(nc, weights, xT, x, edge_rows, edge_pair, type_weights, bias_T, bias_rows, out):
    f32, f32r, bf16 = mybir.dt.float32, mybir.dt.float32r, mybir.dt.bfloat16
    i32, i16 = mybir.dt.int32, mybir.dt.int16
    ALU, ACT, AX = mybir.AluOpType, mybir.ActivationFunctionType, mybir.AxisListType
    SCALE = float(HEAD_DIM) ** -0.5
    GROUP = HEADS_PER_GROUP * NODES

    with ExitStack() as ctx:
        def sb(name, shape, dt):
            return ctx.enter_context(nc.sbuf_tensor(name, shape, dt))

        def sem(name):
            return ctx.enter_context(nc.semaphore(name))

        raw = sb("raw", [P, RAW_SLOTS, QUARTER], f32)
        high = sb("high", [P, SPLIT_SLOTS, FEATURES], f32r)
        low = sb("low", [P, SPLIT_SLOTS, FEATURES], f32r)
        full_op = [sb(f"full_op{s}", [P, SPAN], f32) for s in range(3)]
        high_op = [sb(f"high_op{s}", [P, SPAN], f32r) for s in range(3)]
        low_op = [sb(f"low_op{s}", [P, SPAN], f32r) for s in range(3)]
        area = sb("area", [P, 10368], f32)
        mask_hot = area[:, 0:4608].bitcast(bf16)
        count_hot = area[:, 4608:9216].bitcast(bf16)
        src_hot = area[:, 9216:10368].bitcast(bf16)
        pair_i = area[0:2, 0:3072].bitcast(i32)
        pair_b = area[0:2, 3072:4608].bitcast(bf16)
        probs = area[0:NODES, 0:1536]
        probs_T = area[0:NODES, 1536:3072]
        v2 = area[0:NODES, 3072:4096]
        means = area[:, 0:RELATIONS * SPAN]
        tanh_u = area[0:NODES, 6144:7168]
        tanh_less_x = area[0:NODES, 7168:8192]
        twice_x1 = area[0:NODES, 8192:9216]
        natural = sb("natural", [NODES, FEATURES], f32)
        resid = sb("resid", [NODES, FEATURES], f32)
        x1 = sb("x1", [NODES, FEATURES], f32)
        x1_high = sb("x1_high", [NODES, FEATURES], f32r)
        x1_low = sb("x1_low", [NODES, FEATURES], f32r)
        counts = sb("counts", [NODES, RELATIONS * NODES], f32r)
        adj_high = sb("adj_high", [NODES, RELATIONS * NODES], f32r)
        adj_low = sb("adj_low", [NODES, RELATIONS * NODES], f32r)
        adj = area[0:NODES, 9216:9984]
        hi_count = sb("hi_count", [NODES, GROUP], f32)
        rows = sb("rows", [65, FEATURES], f32)
        biases = sb("biases", [P, 6, CHUNKS], f32)
        ident = sb("ident", [P, P], f32)
        ident_b = sb("ident_b", [P, P], bf16)
        ones = sb("ones", [P, P], f32)
        ones_r = sb("ones_r", [NODES, NODES], f32r)
        not_later = sb("not_later", [P, 4, P], bf16)
        key_w = sb("key_w", [2, P], bf16)
        neg_key_w = sb("neg_key_w", [2, P], bf16)
        index = sb("index", [P, CLASSES * NODES], i16)
        powers = sb("powers", [P, EDGE_CHUNKS], i16)
        edge_i = sb("edge_i", [4 * EDGE_CHUNKS, P], i32)
        edge_f = sb("edge_f", [4 * EDGE_CHUNKS, P], f32)
        edge_c = sb("edge_c", [P, 4, EDGE_CHUNKS], f32)
        nearest = sb("nearest", [P, EDGE_CHUNKS], f32)
        mask_at = sb("mask_at", [P, EDGE_CHUNKS], f32)
        mask_w = sb("mask_w", [P, EDGE_CHUNKS], f32)
        count_at = sb("count_at", [P, EDGE_CHUNKS], f32)
        count_w = sb("count_w", [P, EDGE_CHUNKS], f32)
        tmp_a = sb("tmp_a", [P, EDGE_CHUNKS], f32)
        tmp_b = sb("tmp_b", [P, EDGE_CHUNKS], f32)
        kind = sb("kind", [NODES, CLASSES], f32)
        kind_abs = sb("kind_abs", [NODES, CLASSES], f32)
        kind_exp = sb("kind_exp", [NODES, CLASSES], f32)
        kind_log = sb("kind_log", [NODES, CLASSES], f32)
        kind_bias = sb("kind_bias", [NODES, CLASSES], f32)
        last_bits = sb("last_bits", [NODES, CLASSES, NODES], f32)
        newest = sb("newest", [NODES, NODES], f32)
        newest_c = sb("newest_c", [NODES, NODES], f32)
        mask = sb("mask", [NODES, NODES], f32)
        neg_max = sb("neg_max", [NODES, HEADS], f32)
        exp_sum = sb("exp_sum", [NODES, HEADS], f32)
        exp_inv = sb("exp_inv", [NODES, HEADS], f32)
        stats = sb("stats", [NODES, 2, HALVES, 6], f32)
        moments = sb("moments", [NODES, 2, 2], f32)
        std = sb("std", [NODES, 2], f32)
        rstd = sb("rstd", [NODES, 2], f32)
        eps = sb("eps", [NODES, 1], f32)

        psum = ctx.enter_context(nc.psum_tensor("psum", [P, 8, BANK], f32))
        ACC = [0, 2]
        TR = 4
        U = 4
        SCORE_BANKS = [2, 3, 7, 6]
        PV_BANKS = [4, 5, 2, 3]
        MEAN_BANKS = [(2, 3), (6, 7)]

        def span(t):
            return psum[:, t:t + 2, 0:SPAN // 2]

        raw_in = [sem(f"raw_in{n}") for n in range(RAW_SLOTS)]
        split_free = sem("split_free")
        high_ready = sem("high_ready")
        low_ready = sem("low_ready")
        direct_used = sem("direct_used")
        full_ready = sem("full_ready")
        high_op_ready = sem("high_op_ready")
        op_ready = [sem(f"op_ready{s}") for s in range(3)]
        natural_ready = sem("natural_ready")
        transposed = sem("transposed")
        xT_in, pair_in, edges_in = sem("xT_in"), sem("pair_in"), sem("edges_in")
        kinds_in, biases_in, x_in, rows_in = sem("kinds_in"), sem("biases_in"), sem("x_in"), sem("rows_in")
        consts = sem("consts")
        pair_ready = sem("pair_ready")
        edge_f_ready = sem("edge_f_ready")
        keys_ready = sem("keys_ready")
        keys_used = sem("keys_used")
        hot_ready = sem("hot_ready")
        bits_ready, bits_copied = sem("bits_ready"), sem("bits_copied")
        kind_a, kind_e, kind_l = sem("kind_a"), sem("kind_e"), sem("kind_l")
        scores_ready = sem("scores_ready")
        max_ready = sem("max_ready")
        exp_ready = sem("exp_ready")
        probs_ready = sem("probs_ready")
        probs_T_ready = sem("probs_T_ready")
        probs_T_copied = sem("probs_T_copied")
        v2_ready = sem("v2_ready")
        pv_ready = sem("pv_ready")
        counts_packed, counts_ready = sem("counts_packed"), sem("counts_ready")
        degree_ready = sem("degree_ready")
        adj_ready, adj_high_ready, adj_low_ready = sem("adj_ready"), sem("adj_high_ready"), sem("adj_low_ready")
        var_ready, std_ready = sem("var_ready"), sem("std_ready")
        x1_ready, x1_high_ready, x1_low_ready = sem("x1_ready"), sem("x1_high_ready"), sem("x1_low_ready")
        mean_sum = sem("mean_sum")
        mean_out = [sem("mean_out_scalar"), sem("mean_out_vector")]
        tanh_ready = sem("tanh_ready")
        z_ready = sem("z_ready")
        out_ready = sem("out_ready")
        out_done = sem("out_done")
        dve_step = sem("dve_step")

        X_OP = 2

        block = ctx.enter_context(nc.Block())

        @block.sync
        def _(sp):
            sp.dma_start(full_op[X_OP][:, :], xT).then_inc(xT_in, 16)
            for slot in range(RAW_SLOTS):
                sp.dma_start(raw[:, slot, :], weights[slot, :, :]).then_inc(raw_in[slot], 16)
            with sp.Fori(1, MATRICES // 2) as pair:
                for slot in range(RAW_SLOTS):
                    parity, quarter = divmod(slot, QUARTERS)
                    if quarter == 0:
                        sp.wait_ge(direct_used, pair * 2 - 1 + parity)
                    else:
                        sp.wait_ge(low_ready, pair * (2 * SPLITS) + SPLITS * parity
                                   + CHUNKS_PER_QUARTER * quarter - 2 * SPLITS)
                    src = weights[bass.ds(pair * RAW_SLOTS + slot, 1), :, :].rearrange("a p n -> (a p) n")
                    sp.dma_start(raw[:, slot, :], src).then_inc(raw_in[slot], 16)
            for half in range(HALVES):
                sp.wait_ge(out_ready, half + 1)
                cols = slice(half * BANK, (half + 1) * BANK)
                sp.dma_start(out[:, cols], resid[:, cols]).then_inc(out_done, 16)
            sp.wait_ge(out_done, 16 * HALVES)

        @block.gpsimd
        def _(pool):
            nc.gpsimd.iota(key_w[:, :], [[0, P]], base=NODES, channel_multiplier=1 - NODES,
                           allow_small_or_imprecise_dtypes=True).then_inc(split_free, SPLIT_SLOTS)
            nc.gpsimd.iota(neg_key_w[:, :], [[0, P]], base=-NODES, channel_multiplier=NODES - 1,
                           allow_small_or_imprecise_dtypes=True)
            nc.gpsimd.memset(ident[:, :], 0.0)
            nc.gpsimd.memset(not_later[:, :, :], BIG_KEY).then_inc(consts, 1)
            pool.wait_ge(consts, 1)
            nc.gpsimd.affine_select(out=ident[:, :], in_=ident[:, :], compare_op=ALU.not_equal, fill=1.0,
                                    base=0, pattern=[[-1, P]], channel_multiplier=1).then_inc(consts, 1)
            nc.gpsimd.affine_select(out=not_later[:, :, :], in_=not_later[:, :, :], compare_op=ALU.is_ge,
                                    fill=0.0, base=0, pattern=[[0, 4], [-1, P]],
                                    channel_multiplier=1).then_inc(consts, 1)
            pool.wait_ge(consts, 3)
            nc.gpsimd.tensor_copy(ident_b[:, :], ident[:, :]).then_inc(consts, 1)
            nc.gpsimd.iota(index[:, :], [[1, CLASSES * NODES]], base=0, channel_multiplier=0,
                           allow_small_or_imprecise_dtypes=True)
            nc.gpsimd.iota(powers[:, :], [[P, EDGE_CHUNKS]], base=127 * P, channel_multiplier=0,
                           allow_small_or_imprecise_dtypes=True)
            nc.gpsimd.memset(ones[:, :], 1.0)
            nc.gpsimd.memset(ones_r[:, :].bitcast(f32), 1.0)
            nc.gpsimd.memset(eps[:, :], EPS).then_inc(consts, 1)

        CONST_IDENT, CONST_KEYS, CONST_ALL = 3, 4, 5

        @block.scalar
        def _(act):
            act.dma_start(pair_i, edge_pair).then_inc(pair_in, 16)
            act.dma_start(edge_i[:, :], edge_rows).then_inc(edges_in, 16)
            act.dma_start(kind[:, :], type_weights).then_inc(kinds_in, 16)
            act.dma_start(biases[:, :, :], bias_T).then_inc(biases_in, 16)
            act.dma_start(resid[:, :], x).then_inc(x_in, 16)
            for r in range(3):
                act.dma_start(rows[32 * r:32 * r + 1, :], bias_rows[r:r + 1, :]).then_inc(rows_in, 16)

            def split_high(parity, arrivals, base, chunks, direct=0):
                quarters = [q for q in range(QUARTERS) if q != direct]
                for c in chunks:
                    quarter, k = quarters[c // CHUNKS_PER_QUARTER], c % CHUNKS_PER_QUARTER
                    slot = parity * QUARTERS + quarter
                    if k == 0:
                        act.wait_ge(raw_in[slot], arrivals)
                    act.wait_ge(split_free, base + c + 1)
                    nc.scalar.copy(high[:, (parity * SPLITS + c) % SPLIT_SLOTS, :],
                                   raw[:, slot, k * FEATURES:(k + 1) * FEATURES]).then_inc(high_ready, 1)

            def copy_natural(bank, done, n):
                act.wait_ge(split_free, done)
                act.wait_ge(transposed, n + 1)
                nc.scalar.copy(natural[:, :].rearrange("n (b f) -> n b f", b=HALVES),
                               psum[0:NODES, bank:bank + 2, :]).then_inc(natural_ready, 1)

            def high_operand(s, n):
                act.wait_ge(full_ready, n + 1)
                nc.scalar.copy(high_op[s][:, :], full_op[s][:, :]).then_inc(high_op_ready, 1)

            act.wait_ge(xT_in, 16)
            for s in (0, 1, X_OP):
                nc.scalar.copy(high_op[s][:, :], full_op[X_OP][:, :]).then_inc(high_op_ready, 1)
            act.wait_ge(pair_in, 16)
            nc.scalar.copy(pair_b, pair_i).then_inc(pair_ready, 1)
            act.wait_ge(kind_a, 1)
            nc.scalar.activation(kind_exp[:, :], kind_abs[:, :], ACT.Exp, scale=-1.0).then_inc(kind_e, 1)
            act.wait_ge(kind_e, 1)
            act.wait_ge(consts, CONST_ALL)
            nc.scalar.activation(kind_log[:, :], kind_exp[:, :], ACT.Ln,
                                 bias=ones[0:NODES, 0:1]).then_inc(kind_l, 1)

            with act.Fori(0, 2) as trip:
                arrivals = trip * 16 + 16
                base = trip * (2 * SPLITS)
                split_high(0, arrivals, base, range(SPLITS))
                copy_natural(ACC[0], base + (SPLIT_SLOTS + SPLITS), trip * 2)
                split_high(1, arrivals, base + SPLITS, range(2))
                high_operand(0, trip * 2 + 1)
                split_high(1, arrivals, base + SPLITS, range(2, SPLITS))
                copy_natural(ACC[1], base + (SPLIT_SLOTS + 2 * SPLITS), trip * 2 + 1)
                high_operand(1, trip * 2 + 2)
            split_high(0, 48, 4 * SPLITS, range(SPLITS))
            copy_natural(ACC[0], SPLIT_SLOTS + 5 * SPLITS, 4)
            act.wait_ge(bits_ready, 1)
            nc.scalar.copy(last_bits[:, :, :], psum[0:NODES, 6, 0:GROUP].rearrange(
                "s (k d) -> s k d", k=CLASSES)).then_inc(bits_copied, 1)
            split_high(1, 48, 5 * SPLITS, range(1))
            high_operand(X_OP, 5)
            split_high(1, 48, 5 * SPLITS, range(1, 4))

            def exponentials(group):
                act.wait_ge(max_ready, group + 1)
                for h in range(group * HEADS_PER_GROUP, (group + 1) * HEADS_PER_GROUP):
                    cols = slice(h * NODES, (h + 1) * NODES)
                    last = nc.scalar.activation(probs[:, cols], probs[:, cols], ACT.Exp,
                                                bias=neg_max[:, h:h + 1], accum_out=exp_sum[:, h:h + 1])
                last.then_inc(exp_ready, 1)

            exponentials(0)
            exponentials(1)
            split_high(1, 48, 5 * SPLITS, range(4, 5))
            exponentials(2)
            exponentials(3)
            split_high(1, 48, 5 * SPLITS, range(5, 6))
            act.wait_ge(split_free, SPLIT_SLOTS + 6 * SPLITS)
            nc.scalar.copy(v2.rearrange("n (b f) -> n b f", b=HALVES),
                           psum[0:NODES, ACC[0]:ACC[0] + 2, :]).then_inc(v2_ready, 1)
            for group in (1, 3):
                act.wait_ge(probs_T_ready, group + 1)
                nc.scalar.copy(probs_T[:, group * GROUP:(group + 1) * GROUP],
                               psum[0:NODES, SCORE_BANKS[group], 0:GROUP]).then_inc(probs_T_copied, 1)
            split_high(0, 64, 6 * SPLITS, range(2))
            high_operand(0, 6)
            split_high(0, 64, 6 * SPLITS, range(2, SPLITS))
            act.wait_ge(adj_ready, 1)
            nc.scalar.copy(adj_high[:, :], adj).then_inc(adj_high_ready, 1)
            split_high(1, 64, 7 * SPLITS, range(2))
            act.wait_ge(var_ready, 1)
            nc.scalar.activation(std[:, 0:1], moments[:, 0, 1:2], ACT.Sqrt, bias=eps[:, :]).then_inc(std_ready, 1)
            act.wait_ge(x1_ready, 1)
            nc.scalar.copy(x1_high[:, :], x1[:, :]).then_inc(x1_high_ready, 1)
            high_operand(1, 7)
            means_v = means.rearrange("p (r k d) -> p r k d", r=RELATIONS, k=CHUNKS)
            for k in range(CHUNKS):
                act.wait_ge(mean_sum, k + 1)
                nc.scalar.copy(means_v[:, 0:4, k, :], psum[:, MEAN_BANKS[k % 2][0], 0:GROUP].rearrange(
                    "p (r d) -> p r d", r=4)).then_inc(mean_out[0], 1)
            split_high(1, 64, 7 * SPLITS, range(2, SPLITS))
            split_high(0, 80, 8 * SPLITS, range(SPLITS))

            def mean_operand(s, relation, used):
                act.wait_ge(split_free, used)
                mean = means[:, bass.ds(relation * SPAN, SPAN)]
                nc.scalar.copy(full_op[s][:, 0:CHUNKS_PER_QUARTER * NODES],
                               means[:, bass.ds(relation * SPAN, CHUNKS_PER_QUARTER * NODES)])
                nc.scalar.copy(high_op[s][:, :], mean).then_inc(high_op_ready, 1)

            act.wait_ge(mean_out[1], CHUNKS)
            act.wait_ge(mean_out[0], CHUNKS)
            with act.Fori(0, RELATIONS // 2) as trip:
                base = trip * (2 * SPLITS) + REL0 * SPLITS
                mean_operand(0, trip * 2, base + (SPLIT_SLOTS - SPLITS))
                split_high(1, trip * 16 + 80, base, range(SPLITS))
                mean_operand(1, trip * 2 + 1, base + SPLIT_SLOTS)
                split_high(0, trip * 16 + 96, base + SPLITS, range(SPLITS))
            copy_natural(U, SPLIT_SLOTS + GATE_U * SPLITS, 6)
            split_high(1, 16 * 9, GATE_U * SPLITS, range(1), direct=3)
            high_operand(0, 8)
            split_high(1, 16 * 9, GATE_U * SPLITS, range(1, 4), direct=3)
            nc.scalar.activation(tanh_u.rearrange("n (b f) -> n b f", b=HALVES), psum[0:NODES, U:U + 2, :],
                                 ACT.Tanh).then_inc(tanh_ready, 1)
            split_high(1, 16 * 9, GATE_U * SPLITS, range(4, SPLITS), direct=3)
            act.wait_ge(var_ready, 2)
            nc.scalar.activation(std[:, 1:2], moments[:, 1, 1:2], ACT.Sqrt, bias=eps[:, :]).then_inc(std_ready, 1)

        @block.vector
        def _(dve):
            steps = [0]

            def step(instruction):
                steps[0] += 1
                instruction.then_inc(dve_step, 1)

            def split_low(parity, base, chunks, direct=0):
                quarters = [q for q in range(QUARTERS) if q != direct]
                for c in chunks:
                    slot = parity * QUARTERS + quarters[c // CHUNKS_PER_QUARTER]
                    k, ring = c % CHUNKS_PER_QUARTER, (parity * SPLITS + c) % SPLIT_SLOTS
                    dve.wait_ge(high_ready, base + c + 1)
                    nc.vector.tensor_tensor(low[:, ring, :], raw[:, slot, k * FEATURES:(k + 1) * FEATURES],
                                            high[:, ring, :].bitcast(f32), ALU.subtract).then_inc(low_ready, 1)

            def low_operand(s, n):
                dve.wait_ge(high_op_ready, n)
                nc.vector.tensor_tensor(low_op[s][:, :], full_op[s][:, :], high_op[s][:, :].bitcast(f32),
                                        ALU.subtract).then_inc(op_ready[s], 1)

            def wide(ap):
                return ap.rearrange("p (b k d) -> p b k d", b=2, k=CHUNKS // 2)

            def transposed_psum(bank):
                return span(bank).rearrange("p b (k d) -> p b k d", k=CHUNKS // 2)

            def biased_operand(s, n, bias):
                dve.wait_ge(transposed, n + 1)
                nc.vector.tensor_tensor(
                    wide(full_op[s][:, :]), transposed_psum(TR),
                    bias.rearrange("p a (b k) -> p (a b) k", b=2).unsqueeze(3)
                    .broadcast_to([P, 2, CHUNKS // 2, NODES]), ALU.add).then_inc(full_ready, 1)

            dve.wait_ge(xT_in, 16)
            for s in (0, 1):
                last = nc.vector.tensor_copy(full_op[s][:, :], full_op[X_OP][:, :])
            last.then_inc(full_ready, 1)
            for n, s in enumerate((0, 1, X_OP)):
                dve.wait_ge(high_op_ready, n + 1)
                nc.vector.tensor_tensor(low_op[s][:, :], full_op[X_OP][:, :], high_op[s][:, :].bitcast(f32),
                                        ALU.subtract).then_inc(op_ready[s], 1)
            dve.wait_ge(edges_in, 16)
            nc.vector.tensor_copy(edge_f[:, :], edge_i[:, :]).then_inc(edge_f_ready, 1)
            dve.wait_ge(kinds_in, 16)
            nc.vector.scalar_tensor_tensor(kind_abs[:, :], kind[:, :], -1.0, kind[:, :],
                                           ALU.mult, ALU.max).then_inc(kind_a, 1)
            dve.wait_ge(transposed, 1)
            step(nc.vector.tensor_copy(edge_c[:, :, :], psum[:, 6, 0:4 * EDGE_CHUNKS].rearrange(
                "p (a c) -> p a c", a=4)))
            for bank in range(EDGE_CHUNKS // 4):
                dve.wait_ge(keys_ready, bank + 1)
                nc.vector.tensor_reduce(nearest[:, 4 * bank:4 * bank + 4],
                                        psum[:, bank + 2, :].rearrange("p (c j) -> p c j", c=4),
                                        axis=AX.X, op=ALU.min, apply_absolute_value=True).then_inc(keys_used, 1)
            src_c, dst_c, type5_c, type8_c = (edge_c[:, n, :] for n in range(4))
            dve.wait_ge(consts, CONST_ALL)
            dve.wait_ge(dve_step, steps[0])
            step(nc.vector.tensor_scalar(tmp_a[:, :], type5_c, 0.0, float(CLASSES * NODES), ALU.is_equal, ALU.mult))
            step(nc.vector.scalar_tensor_tensor(tmp_b[:, :], type5_c, float(NODES), dst_c, ALU.mult, ALU.add))
            step(nc.vector.tensor_scalar(count_at[:, :], type8_c, 4.0, None, ALU.is_ge))
            dve.wait_ge(keys_used, EDGE_CHUNKS // 4)
            step(nc.vector.scalar_tensor_tensor(mask_w[:, :], nearest[:, :], 0.0, powers[:, :].bitcast(bf16),
                                                ALU.is_gt, ALU.mult))
            dve.wait_ge(dve_step, steps[0])
            step(nc.vector.scalar_tensor_tensor(mask_at[:, :], tmp_b[:, :], -float(NODES), tmp_a[:, :],
                                                ALU.add, ALU.add))
            step(nc.vector.tensor_scalar(count_w[:, :], count_at[:, :], PACK - 1.0, 1.0, ALU.mult, ALU.add))
            dve.wait_ge(dve_step, steps[0])
            step(nc.vector.scalar_tensor_tensor(tmp_a[:, :], count_at[:, :], -4.0, type8_c, ALU.mult, ALU.add))
            dve.wait_ge(dve_step, steps[0])
            step(nc.vector.scalar_tensor_tensor(count_at[:, :], tmp_a[:, :], float(NODES), dst_c, ALU.mult, ALU.add))
            dve.wait_ge(kind_l, 1)
            step(nc.vector.scalar_tensor_tensor(kind_bias[:, :], kind[:, :], 0.0, kind_log[:, :], ALU.max, ALU.add))
            dve.wait_ge(dve_step, steps[0])
            dve.wait_ge(biases_in, 16)

            with dve.Fori(0, 2) as trip:
                base = trip * (2 * SPLITS)
                split_low(0, base, range(SPLITS))
                split_low(1, base + SPLITS, range(2))
                for j in range(2):
                    biased_operand(j, trip * 2 + j + 1, biases[:, bass.ds(trip * 2 + j, 1), :])
                    low_operand(j, trip * 2 + 4 + j)
                    if j == 0:
                        split_low(1, base + SPLITS, range(2, SPLITS))
                    with dve.Fori(0, EDGE_CHUNKS // 4) as i:
                        chunk = trip * (EDGE_CHUNKS // 2) + i + j * (EDGE_CHUNKS // 4)
                        def column(t):
                            return t[:, bass.ds(chunk, 1)]
                        nc.vector.tensor_scalar(src_hot[:, bass.ds(chunk * NODES, NODES)], index[:, 0:NODES],
                                                edge_c[:, 0, bass.ds(chunk, 1)], None, ALU.is_equal)
                        nc.vector.tensor_scalar(mask_hot[:, bass.ds(chunk * GROUP, GROUP)], index[:, :],
                                                column(mask_at), column(mask_w), ALU.is_equal, ALU.mult)
                        nc.vector.tensor_scalar(count_hot[:, bass.ds(chunk * GROUP, GROUP)], index[:, :],
                                                column(count_at), column(count_w), ALU.is_equal,
                                                ALU.mult).then_inc(hot_ready, 1)
            split_low(0, 4 * SPLITS, range(SPLITS))
            biased_operand(X_OP, 5, biases[:, 4:5, :])
            split_low(1, 5 * SPLITS, range(1))
            low_operand(X_OP, 8)

            dve.wait_ge(bits_copied, 1)
            step(nc.vector.scalar_tensor_tensor(last_bits[:, 3, :], ident[0:NODES, 0:NODES], 0.5,
                                                last_bits[:, 3, :], ALU.mult, ALU.max))
            dve.wait_ge(dve_step, steps[0])
            step(nc.vector.tensor_reduce(newest[:, :], last_bits[:, :, :].rearrange("s k d -> s d k"),
                                         axis=AX.X, op=ALU.max))
            dve.wait_ge(dve_step, steps[0])
            step(nc.vector.tensor_scalar(mask[:, :], newest[:, :], 0.0, NO_EDGE, ALU.is_equal, ALU.mult))
            step(nc.vector.tensor_scalar(newest_c[:, :], newest[:, :], 0.25, None, ALU.max))
            dve.wait_ge(dve_step, steps[0])
            step(nc.vector.tensor_tensor(last_bits[:, :, :], last_bits[:, :, :],
                                         newest_c[:, :].unsqueeze(1).broadcast_to([NODES, CLASSES, NODES]),
                                         ALU.is_equal))
            for k in range(CLASSES):
                dve.wait_ge(dve_step, steps[0])
                step(nc.vector.scalar_tensor_tensor(mask[:, :], last_bits[:, k, :], kind_bias[:, k:k + 1],
                                                    mask[:, :], ALU.mult, ALU.add))
            split_low(1, 5 * SPLITS, range(1, 3))

            def head_view(group):
                return probs[:, group * GROUP:(group + 1) * GROUP].rearrange("n (h m) -> n h m", h=HEADS_PER_GROUP)

            def group_cols(t, group):
                return t[:, group * HEADS_PER_GROUP:(group + 1) * HEADS_PER_GROUP]

            def masked_scores(group):
                dve.wait_ge(scores_ready, group + 1)
                dve.wait_ge(dve_step, steps[0])
                step(nc.vector.scalar_tensor_tensor(
                    head_view(group),
                    psum[0:NODES, SCORE_BANKS[group], 0:GROUP].rearrange("n (h m) -> n h m", h=HEADS_PER_GROUP),
                    SCALE, mask[:, :].unsqueeze(1).broadcast_to([NODES, HEADS_PER_GROUP, NODES]),
                    ALU.mult, ALU.add))
                dve.wait_ge(dve_step, steps[0])
                nc.vector.tensor_reduce(group_cols(neg_max, group), head_view(group), axis=AX.X, op=ALU.max,
                                        negate=True).then_inc(max_ready, 1)

            def normalise(group):
                dve.wait_ge(exp_ready, group + 1)
                step(nc.vector.reciprocal(group_cols(exp_inv, group), group_cols(exp_sum, group)))
                dve.wait_ge(dve_step, steps[0])
                nc.vector.tensor_tensor(
                    head_view(group), head_view(group),
                    group_cols(exp_inv, group).unsqueeze(2).broadcast_to([NODES, HEADS_PER_GROUP, NODES]),
                    ALU.mult).then_inc(probs_ready, 1)

            masked_scores(0)
            masked_scores(1)
            split_low(1, 5 * SPLITS, range(3, 4))
            masked_scores(2)
            masked_scores(3)
            split_low(1, 5 * SPLITS, range(4, 5))
            normalise(0)
            normalise(1)
            split_low(1, 5 * SPLITS, range(5, 6))
            normalise(2)
            normalise(3)
            for group in (0, 2):
                dve.wait_ge(probs_T_ready, group + 1)
                nc.vector.tensor_copy(probs_T[:, group * GROUP:(group + 1) * GROUP],
                                      psum[0:NODES, SCORE_BANKS[group], 0:GROUP]).then_inc(probs_T_copied, 1)
            for i in range(GROUPS):
                dve.wait_ge(pv_ready, i + 1)
                both = psum[:, PV_BANKS[i], 0:4 * NODES].rearrange("p (k h d) -> p k h d", k=2, h=2)
                into = full_op[0][:, :].rearrange("p (k d) -> p k d", k=CHUNKS)
                for h in range(2):
                    part = slice(h * HEAD_DIM, (h + 1) * HEAD_DIM)
                    last = nc.vector.tensor_tensor(
                        into[part, 2 * i:2 * i + 2, :], both[part, :, h, :],
                        biases[part, 5, 2 * i:2 * i + 2].unsqueeze(2).broadcast_to([HEAD_DIM, 2, NODES]), ALU.add)
            last.then_inc(full_ready, 1)
            split_low(0, 6 * SPLITS, range(2))
            low_operand(0, 9)
            counts_f = counts[:, :].bitcast(f32)
            dve.wait_ge(counts_packed, 1)
            packed = psum[0:NODES, 6, 0:GROUP]
            step(nc.vector.tensor_scalar(hi_count[:, :], packed, 1.0 / PACK, 0.375, ALU.mult, ALU.subtract))
            dve.wait_ge(dve_step, steps[0])
            step(nc.vector.tensor_scalar(counts[:, GROUP:2 * GROUP], hi_count[:, :], ROUND, ROUND, ALU.add, ALU.subtract))
            dve.wait_ge(dve_step, steps[0])
            nc.vector.scalar_tensor_tensor(counts[:, 0:GROUP], counts_f[:, GROUP:2 * GROUP], -PACK, packed,
                                           ALU.mult, ALU.add).then_inc(counts_ready, 1)
            split_low(0, 6 * SPLITS, range(2, 4))
            dve.wait_ge(degree_ready, 1)
            step(nc.vector.tensor_scalar(adj[:, 0:GROUP], psum[0:NODES, 7, 0:GROUP], 1.0, None, ALU.max))
            step(nc.vector.tensor_scalar(adj[:, GROUP:2 * GROUP], psum[0:NODES, 2, 0:GROUP], 1.0, None, ALU.max))
            dve.wait_ge(dve_step, steps[0])
            step(nc.vector.reciprocal(adj, adj))
            split_low(0, 6 * SPLITS, range(4, 6))
            dve.wait_ge(dve_step, steps[0])
            dve.wait_ge(counts_ready, 1)
            nc.vector.tensor_tensor(adj, adj, counts_f, ALU.mult).then_inc(adj_ready, 1)
            split_low(1, 7 * SPLITS, range(2))
            dve.wait_ge(adj_high_ready, 1)
            nc.vector.tensor_tensor(adj_low[:, :], adj, adj_high[:, :].bitcast(f32),
                                    ALU.subtract).then_inc(adj_low_ready, 1)

            dve.wait_ge(x_in, 16)
            dve.wait_ge(split_free, SPLIT_SLOTS + 7 * SPLITS)
            for half in range(HALVES):
                cols = slice(half * BANK, (half + 1) * BANK)
                step(nc.vector.tensor_tensor(resid[:, cols], psum[0:NODES, half, :], resid[:, cols], ALU.add))
            for half in range(HALVES):
                cols = slice(half * BANK, (half + 1) * BANK)
                dve.wait_ge(dve_step, steps[0] - 1)
                step(nc.vector.bn_stats(stats[:, 0, half, :], resid[:, cols]))
            dve.wait_ge(dve_step, steps[0])
            nc.vector.bn_aggr(moments[:, 0, :], stats[:, 0, :, :].rearrange("p b s -> p (b s)")).then_inc(var_ready, 1)
            dve.wait_ge(std_ready, 1)
            step(nc.vector.reciprocal(rstd[:, 0:1], std[:, 0:1]))
            dve.wait_ge(var_ready, 1)
            dve.wait_ge(dve_step, steps[0])
            nc.vector.tensor_scalar(x1[:, :], resid[:, :], moments[:, 0, 0:1], rstd[:, 0:1],
                                    ALU.subtract, ALU.mult).then_inc(x1_ready, 1)
            dve.wait_ge(x1_high_ready, 1)
            nc.vector.tensor_tensor(x1_low[:, :], x1[:, :], x1_high[:, :].bitcast(f32),
                                    ALU.subtract).then_inc(x1_low_ready, 1)
            dve.wait_ge(transposed, 7)
            nc.vector.tensor_copy(wide(full_op[1][:, :]), transposed_psum(TR)).then_inc(full_ready, 1)
            low_operand(1, 10)
            means_v = means.rearrange("p (r k d) -> p r k d", r=RELATIONS, k=CHUNKS)
            for k in range(CHUNKS):
                dve.wait_ge(mean_sum, k + 1)
                nc.vector.tensor_copy(means_v[:, 4:8, k, :], psum[:, MEAN_BANKS[k % 2][1], 0:GROUP].rearrange(
                    "p (r d) -> p r d", r=4)).then_inc(mean_out[1], 1)
            split_low(1, 7 * SPLITS, range(2, SPLITS))
            nc.vector.tensor_scalar(twice_x1, x1[:, :], 2.0, None, ALU.mult)
            split_low(0, 8 * SPLITS, range(SPLITS))

            def mean_low_operand(s, relation, n):
                dve.wait_ge(high_op_ready, n)
                nc.vector.tensor_tensor(low_op[s][:, :], means[:, bass.ds(relation * SPAN, SPAN)],
                                        high_op[s][:, :].bitcast(f32), ALU.subtract).then_inc(op_ready[s], 1)

            dve.wait_ge(mean_out[0], CHUNKS)
            dve.wait_ge(mean_out[1], CHUNKS)
            with dve.Fori(0, RELATIONS // 2) as trip:
                base = trip * (2 * SPLITS) + REL0 * SPLITS
                mean_low_operand(0, trip * 2, trip * 2 + 11)
                split_low(1, base, range(SPLITS))
                mean_low_operand(1, trip * 2 + 1, trip * 2 + 12)
                split_low(0, base + SPLITS, range(SPLITS))
            split_low(1, GATE_U * SPLITS, range(1), direct=3)
            dve.wait_ge(transposed, 8)
            nc.vector.tensor_copy(wide(full_op[0][:, :]),
                                  span(2).rearrange("p b (k d) -> p b k d", k=CHUNKS // 2)).then_inc(full_ready, 1)
            low_operand(0, 19)
            split_low(1, GATE_U * SPLITS, range(1, 4), direct=3)
            dve.wait_ge(tanh_ready, 1)
            step(nc.vector.tensor_tensor(tanh_less_x, tanh_u, x1[:, :], ALU.subtract))
            split_low(1, GATE_U * SPLITS, range(4, SPLITS), direct=3)
            for half in range(HALVES):
                cols = slice(half * BANK, (half + 1) * BANK)
                dve.wait_ge(dve_step, steps[0])
                dve.wait_ge(z_ready, half + 1)
                step(nc.vector.tensor_tensor(resid[:, cols], psum[0:NODES, half, :], tanh_less_x[:, cols], ALU.mult))
                dve.wait_ge(dve_step, steps[0])
                step(nc.vector.tensor_tensor(resid[:, cols], resid[:, cols], twice_x1[:, cols], ALU.add))
                dve.wait_ge(dve_step, steps[0])
                step(nc.vector.bn_stats(stats[:, 1, half, :], resid[:, cols]))
            dve.wait_ge(dve_step, steps[0])
            nc.vector.bn_aggr(moments[:, 1, :], stats[:, 1, :, :].rearrange("p b s -> p (b s)")).then_inc(var_ready, 1)
            dve.wait_ge(std_ready, 2)
            step(nc.vector.reciprocal(rstd[:, 1:2], std[:, 1:2]))
            dve.wait_ge(var_ready, 2)
            dve.wait_ge(dve_step, steps[0])
            for half in range(HALVES):
                cols = slice(half * BANK, (half + 1) * BANK)
                nc.vector.tensor_scalar(resid[:, cols], resid[:, cols], moments[:, 1, 0:1], rstd[:, 1:2],
                                        ALU.subtract, ALU.mult).then_inc(out_ready, 1)

        @block.tensor
        def _(pe):
            def add(into, lhsT, rhs, start=False, stop=False):
                return nc.tensor.matmul(into, lhsT, rhs, start=start, stop=stop, skip_group_check=True)

            def product(parity, arrivals, base, s, acc, opened=False, direct=0, ends=True, between=None):
                c = 0
                for quarter in range(QUARTERS):
                    slot = parity * QUARTERS + quarter
                    first = quarter == 0 and not opened
                    final = quarter == QUARTERS - 1 and ends
                    if quarter == direct:
                        pe.wait_ge(raw_in[slot], arrivals)
                        order = [(k, b) for k in range(CHUNKS_PER_QUARTER) for b in range(HALVES)]
                        if final:
                            order.sort(key=lambda kb: kb[1])
                        for k, b in order:
                            chunk = quarter * CHUNKS_PER_QUARTER + k
                            at = k * FEATURES + b * BANK
                            last = add(psum[0:NODES, acc + b, :], full_op[s][:, chunk * NODES:(chunk + 1) * NODES],
                                       raw[:, slot, at:at + BANK], start=first and k == 0,
                                       stop=final and k == CHUNKS_PER_QUARTER - 1)
                            if final and k == CHUNKS_PER_QUARTER - 1:
                                last.then_inc(z_ready, 1)
                        if not final:
                            last.then_inc(direct_used, 1)
                    else:
                        for k in range(CHUNKS_PER_QUARTER):
                            chunk = quarter * CHUNKS_PER_QUARTER + k
                            nodes = slice(chunk * NODES, (chunk + 1) * NODES)
                            ring = (parity * SPLITS + c) % SPLIT_SLOTS
                            pe.wait_ge(low_ready, base + c + 1)
                            for lhsT, rhs in ((high_op, high), (low_op, high), (high_op, low)):
                                for b in range(HALVES):
                                    last = add(psum[0:NODES, acc + b, :], lhsT[s][:, nodes],
                                               rhs[:, ring, b * BANK:(b + 1) * BANK],
                                               start=first and k == 0 and lhsT is high_op and rhs is high,
                                               stop=final and k == CHUNKS_PER_QUARTER - 1 and rhs is low)
                            last.then_inc(split_free, 1)
                            c += 1
                    if quarter == 0 and between:
                        between()

            def transpose_natural(n, bank, source, f32_before):
                if n is not None:
                    pe.wait_ge(natural_ready, n)
                pe.wait_ge(full_ready, f32_before + 1)
                for k in range(CHUNKS):
                    b, at = divmod(k, CHUNKS // 2)
                    last = nc.tensor.transpose(psum[:, bank + b, at * NODES:(at + 1) * NODES],
                                               source[:, k * P:(k + 1) * P], ident[0:NODES, 0:NODES])
                last.then_inc(transposed, 1)

            def open_with_bias(acc, row):
                at = 32 * row
                for b in range(HALVES):
                    add(psum[0:NODES, acc + b, :], ones[at:at + 1, 0:NODES],
                        rows[at:at + 1, b * BANK:(b + 1) * BANK], start=True)

            pe.wait_ge(consts, CONST_IDENT)
            pe.wait_ge(edge_f_ready, 1)
            nc.tensor.transpose(psum[:, 6, 0:4 * EDGE_CHUNKS], edge_f[:, :],
                                ident[0:4 * EDGE_CHUNKS, 0:4 * EDGE_CHUNKS]).then_inc(transposed, 1)
            pe.wait_ge(consts, CONST_KEYS)
            pe.wait_ge(pair_ready, 1)
            pe.wait_ge(dve_step, 1)
            for bank in range(EDGE_CHUNKS // 4):
                into = psum[:, bank + 2, :]
                add(into, key_w[:, :], pair_b[:, bank * BANK:(bank + 1) * BANK], start=True)
                for j in range(4):
                    edges = slice(bank * BANK + j * P, bank * BANK + (j + 1) * P)
                    add(into[:, j * P:(j + 1) * P], pair_b[:, edges], neg_key_w[:, :])
                last = add(into, ident_b[:, :], not_later[:, :, :].rearrange("p c j -> p (c j)"), stop=True)
                last.then_inc(keys_ready, 1)

            with pe.Fori(0, 2) as trip:
                arrivals = trip * 16 + 16
                base = trip * (2 * SPLITS)
                pe.wait_ge(op_ready[0], trip + 1)
                product(0, arrivals, base, 0, ACC[0])
                pe.wait_ge(keys_used, EDGE_CHUNKS // 4)
                pe.wait_ge(op_ready[1], trip + 1)
                product(1, arrivals, base + SPLITS, 1, ACC[1],
                        between=lambda: transpose_natural(trip * 2 + 1, TR, natural, trip * 2))
                transpose_natural(trip * 2 + 2, TR, natural, trip * 2 + 1)
            pe.wait_ge(op_ready[X_OP], 1)
            product(0, 48, 4 * SPLITS, X_OP, ACC[0])
            pe.wait_ge(hot_ready, EDGE_CHUNKS)
            for c in range(EDGE_CHUNKS):
                last = add(psum[0:NODES, 6, 0:GROUP], src_hot[:, c * NODES:(c + 1) * NODES],
                           mask_hot[:, c * GROUP:(c + 1) * GROUP], start=c == 0, stop=c == EDGE_CHUNKS - 1)
            last.then_inc(bits_ready, 1)
            transpose_natural(5, TR, natural, 4)
            pe.wait_ge(op_ready[0], 3)
            pe.wait_ge(op_ready[1], 3)
            for group in range(GROUPS):
                if SCORE_BANKS[group] == 6:
                    pe.wait_ge(bits_copied, 1)
                part = slice(group % 2 * HEAD_DIM, (group % 2 + 1) * HEAD_DIM)
                for j in range(HEADS_PER_GROUP):
                    chunk, at = group // 2 * HEADS_PER_GROUP + j, j * NODES
                    nodes = slice(chunk * NODES, (chunk + 1) * NODES)
                    last = add(psum[0:NODES, SCORE_BANKS[group], at:at + NODES], full_op[1][part, nodes],
                               full_op[0][part, nodes], start=True, stop=True)
                last.then_inc(scores_ready, 1)
            pe.wait_ge(op_ready[X_OP], 2)
            product(1, 48, 5 * SPLITS, X_OP, ACC[0])
            for group in range(GROUPS):
                pe.wait_ge(probs_ready, group + 1)
                for j in range(HEADS_PER_GROUP):
                    at = j * NODES
                    last = nc.tensor.transpose(psum[0:NODES, SCORE_BANKS[group], at:at + NODES],
                                               probs[:, group * GROUP + at:group * GROUP + at + NODES],
                                               ident[0:NODES, 0:NODES])
                last.then_inc(probs_T_ready, 1)
            pe.wait_ge(v2_ready, 1)
            pe.wait_ge(probs_T_copied, GROUPS)
            by_chunk = probs_T.rearrange("m (u p k n) -> m u p k n", u=2, p=2, k=HEADS_PER_GROUP)
            for i in range(GROUPS):
                for k in range(2):
                    chunk = 2 * i + k
                    last = add(psum[:, PV_BANKS[i], k * 2 * NODES:(k + 1) * 2 * NODES],
                               v2[:, chunk * P:(chunk + 1) * P],
                               by_chunk[:, chunk // HEADS_PER_GROUP, :, chunk % HEADS_PER_GROUP, :],
                               start=True, stop=True)
                last.then_inc(pv_ready, 1)
            for c in range(EDGE_CHUNKS):
                last = add(psum[0:NODES, 6, 0:GROUP], src_hot[:, c * NODES:(c + 1) * NODES],
                           count_hot[:, c * GROUP:(c + 1) * GROUP], start=c == 0, stop=c == EDGE_CHUNKS - 1)
            last.then_inc(counts_packed, 1)
            pe.wait_ge(rows_in, 48)
            pe.wait_ge(consts, CONST_ALL)
            open_with_bias(ACC[0], 0)
            pe.wait_ge(op_ready[0], 4)

            def in_degrees():
                pe.wait_ge(counts_ready, 1)
                for half, bank in enumerate((7, 2)):
                    last = add(psum[0:NODES, bank, 0:GROUP], ones_r[:, :],
                               counts[:, half * GROUP:(half + 1) * GROUP], start=True, stop=True)
                last.then_inc(degree_ready, 1)

            product(0, 64, 6 * SPLITS, 0, ACC[0], opened=True, between=in_degrees)
            pe.wait_ge(x1_ready, 1)
            transpose_natural(None, TR, x1, 6)
            pe.wait_ge(adj_low_ready, 1)
            pe.wait_ge(x1_low_ready, 1)
            for k in range(CHUNKS):
                if k >= 2:
                    pe.wait_ge(mean_out[0], k - 1)
                    pe.wait_ge(mean_out[1], k - 1)
                for half in range(2):
                    cols = slice(half * GROUP, (half + 1) * GROUP)
                    into = psum[:, MEAN_BANKS[k % 2][half], 0:GROUP]
                    chunk = slice(k * P, (k + 1) * P)
                    add(into, x1_high[:, chunk], adj_high[:, cols], start=True)
                    add(into, x1_low[:, chunk], adj_high[:, cols])
                    last = add(into, x1_high[:, chunk], adj_low[:, cols], stop=True)
                last.then_inc(mean_sum, 1)
            open_with_bias(ACC[0], 2)
            pe.wait_ge(op_ready[1], 4)
            product(1, 64, 7 * SPLITS, 1, ACC[0], opened=True, ends=False)
            open_with_bias(U, 1)
            product(0, 80, ROOT * SPLITS, 1, U, opened=True, ends=False)
            with pe.Fori(0, RELATIONS // 2) as trip:
                base = trip * (2 * SPLITS) + REL0 * SPLITS
                pe.wait_ge(op_ready[0], trip + 5)
                product(1, trip * 16 + 80, base, 0, U, opened=True)
                pe.wait_ge(op_ready[1], trip + 5)
                product(0, trip * 16 + 96, base + SPLITS, 1, U, opened=True)
            pe.wait_ge(mean_out[0], CHUNKS)
            pe.wait_ge(mean_out[1], CHUNKS)
            transpose_natural(6, 2, natural, 7)
            pe.wait_ge(op_ready[0], 9)
            product(1, 16 * 9, GATE_U * SPLITS, 0, ACC[0], opened=True, direct=3)


def kernel(x, src, dst, edge_type_5, edge_type_8, L0_gnn_edge_type_weights, L0_gnn_wq, L0_gnn_bq, L0_gnn_wk,
           L0_gnn_bk, L0_gnn_wv, L0_gnn_bv, L0_gnn_wiq, L0_gnn_biq, L0_gnn_wik, L0_gnn_bik, L0_gnn_wiv,
           L0_gnn_biv, L0_gnn_wo, L0_gnn_bo, L1_gnn_weight, L1_gnn_root, L1_gnn_bias, L1_gnn_w_gate,
           L1_gnn_b_gate):
    import numpy as np
    import concourse.bacc as bacc
    from concourse import mybir as _mybir
    from concourse.bass_utils import run_bass_kernel_spmd

    def quarters(w):
        return w.reshape(QUARTERS, CHUNKS_PER_QUARTER, P, FEATURES).transpose(0, 2, 1, 3).reshape(
            QUARTERS, P, QUARTER)

    x, src, dst, type5, type8 = (np.asarray(a) for a in (x, src, dst, edge_type_5, edge_type_8))
    w_gate, relations = np.asarray(L1_gnn_w_gate), np.asarray(L1_gnn_weight)
    attention = [np.asarray(w).T for w in (L0_gnn_wk, L0_gnn_wq, L0_gnn_wik, L0_gnn_wiq, L0_gnn_wv, L0_gnn_wiv,
                                           L0_gnn_wo)]
    stream = attention + [w_gate[FEATURES:], np.asarray(L1_gnn_root)] + list(relations) + [w_gate[:FEATURES]]
    biases = [np.asarray(b).reshape(CHUNKS, P).T for b in (L0_gnn_bk, L0_gnn_bq, L0_gnn_bik, L0_gnn_biq,
                                                           L0_gnn_bv, L0_gnn_biv)]
    arrays = {
        "weights": np.concatenate([quarters(w) for w in stream]),
        "xT": x.reshape(NODES, CHUNKS, P).transpose(2, 1, 0).reshape(P, SPAN),
        "x": x,
        "edge_rows": np.concatenate([a.reshape(EDGE_CHUNKS, P) for a in (src, dst, type5, type8)]),
        "edge_pair": np.stack([src, dst]),
        "type_weights": np.broadcast_to(np.asarray(L0_gnn_edge_type_weights), (NODES, CLASSES)),
        "bias_T": np.stack(biases, axis=1),
        "bias_rows": np.stack([np.asarray(b) for b in (L0_gnn_bo, L1_gnn_bias, L1_gnn_b_gate)]),
    }
    nc = bacc.Bacc("TRN2", target_bir_lowering=False, num_devices=1)
    given, args = {}, []
    for name, a in arrays.items():
        given[f"in_{name}"] = np.ascontiguousarray(a)
        args.append(nc.dram_tensor(f"in_{name}", a.shape, _mybir.dt.from_np(a.dtype), kind="ExternalInput").ap())
    out = nc.dram_tensor("out", (NODES, FEATURES), _mybir.dt.float32, kind="ExternalOutput").ap()
    gnn_block(nc, *args, out)
    r = run_bass_kernel_spmd(nc, [given], core_ids=[0])
    return r.results[0]["out"]
```

```python
from contextlib import ExitStack

import concourse.bass as bass
from concourse import mybir

NODES = 96
EDGES = 3072
FEATURES = 1024
HEADS = 16
HEAD_DIM = FEATURES // HEADS
RELATIONS = 8
CLASSES = 4
P = 128
CHUNKS = FEATURES // P
BANK = 512
HALVES = FEATURES // BANK
QUARTERS = 4
CHUNKS_PER_QUARTER = CHUNKS // QUARTERS
QUARTER = CHUNKS_PER_QUARTER * FEATURES
MATRICES = 18
RAW_SLOTS = 2 * QUARTERS
SPLIT_SLOTS = 4
PLAIN = (0, 4)
MIXED = 7
EDGE_CHUNKS = EDGES // P
SPAN = CHUNKS * NODES
K, Q, K2, Q2, V, V2, OUT, GATE_X, ROOT, REL0, GATE_U = (*range(10), MATRICES - 1)
HEADS_PER_GROUP = 4
GROUPS = HEADS // HEADS_PER_GROUP
NO_EDGE = -1.0e30
PACK = 4096.0
BIG_KEY = 16384.0
ROUND = 12582912.0
EPS = 1e-5


def plain_chunks(matrix):
    return PLAIN if matrix < MIXED else ()


def splits(matrix):
    return CHUNKS - len(plain_chunks(matrix))


def splits_before(matrix):
    return sum(splits(m) for m in range(matrix))


def gnn_block(nc, weights, xT, x, edge_rows, edge_pair, type_weights, bias_T, bias_rows, out):
    f32, f32r, bf16 = mybir.dt.float32, mybir.dt.float32r, mybir.dt.bfloat16
    i32, i16 = mybir.dt.int32, mybir.dt.int16
    ALU, ACT, AX = mybir.AluOpType, mybir.ActivationFunctionType, mybir.AxisListType
    SCALE = float(HEAD_DIM) ** -0.5
    GROUP = HEADS_PER_GROUP * NODES

    with ExitStack() as ctx:
        def sb(name, shape, dt):
            return ctx.enter_context(nc.sbuf_tensor(name, shape, dt))

        def sem(name):
            return ctx.enter_context(nc.semaphore(name))

        raw = sb("raw", [P, RAW_SLOTS, QUARTER], f32)
        high = sb("high", [P, SPLIT_SLOTS, FEATURES], f32r)
        low = sb("low", [P, SPLIT_SLOTS, FEATURES], f32r)
        full_op = [sb(f"full_op{s}", [P, SPAN], f32) for s in range(3)]
        high_op = [sb(f"high_op{s}", [P, SPAN], f32r) for s in range(3)]
        low_op = [sb(f"low_op{s}", [P, SPAN], f32r) for s in range(3)]
        area = sb("area", [P, 10368], f32)
        mask_hot = area[:, 0:4608].bitcast(bf16)
        count_hot = area[:, 4608:9216].bitcast(bf16)
        src_hot = area[:, 9216:10368].bitcast(bf16)
        pair_i = area[0:2, 0:3072].bitcast(i32)
        pair_b = area[0:2, 3072:4608].bitcast(bf16)
        probs = area[0:NODES, 0:1536]
        probs_T = area[0:NODES, 1536:3072]
        v2 = area[0:NODES, 3072:4096]
        means = area[:, 0:RELATIONS * SPAN]
        tanh_u = area[0:NODES, 6144:7168]
        tanh_less_x = area[0:NODES, 7168:8192]
        twice_x1 = area[0:NODES, 8192:9216]
        natural = sb("natural", [NODES, FEATURES], f32)
        resid = sb("resid", [NODES, FEATURES], f32)
        x1 = sb("x1", [NODES, FEATURES], f32)
        x1_high = sb("x1_high", [NODES, FEATURES], f32r)
        x1_low = sb("x1_low", [NODES, FEATURES], f32r)
        counts = sb("counts", [NODES, RELATIONS * NODES], f32r)
        adj_high = sb("adj_high", [NODES, RELATIONS * NODES], f32r)
        adj_low = sb("adj_low", [NODES, RELATIONS * NODES], f32r)
        adj = area[0:NODES, 9216:9984]
        hi_count = sb("hi_count", [NODES, GROUP], f32)
        rows = sb("rows", [65, FEATURES], f32)
        biases = sb("biases", [P, 6, CHUNKS], f32)
        ident = sb("ident", [P, P], f32)
        ident_b = sb("ident_b", [P, P], bf16)
        ones = sb("ones", [P, P], f32)
        ones_r = sb("ones_r", [NODES, NODES], f32r)
        not_later = sb("not_later", [P, 4, P], bf16)
        key_w = sb("key_w", [2, P], bf16)
        neg_key_w = sb("neg_key_w", [2, P], bf16)
        index = sb("index", [P, CLASSES * NODES], i16)
        powers = sb("powers", [P, EDGE_CHUNKS], i16)
        edge_i = sb("edge_i", [4 * EDGE_CHUNKS, P], i32)
        edge_f = sb("edge_f", [4 * EDGE_CHUNKS, P], f32)
        edge_c = sb("edge_c", [P, 4, EDGE_CHUNKS], f32)
        nearest = sb("nearest", [P, EDGE_CHUNKS], f32)
        mask_at = sb("mask_at", [P, EDGE_CHUNKS], f32)
        mask_w = sb("mask_w", [P, EDGE_CHUNKS], f32)
        count_at = sb("count_at", [P, EDGE_CHUNKS], f32)
        count_w = sb("count_w", [P, EDGE_CHUNKS], f32)
        tmp_a = sb("tmp_a", [P, EDGE_CHUNKS], f32)
        tmp_b = sb("tmp_b", [P, EDGE_CHUNKS], f32)
        kind = sb("kind", [NODES, CLASSES], f32)
        kind_abs = sb("kind_abs", [NODES, CLASSES], f32)
        kind_exp = sb("kind_exp", [NODES, CLASSES], f32)
        kind_log = sb("kind_log", [NODES, CLASSES], f32)
        kind_bias = sb("kind_bias", [NODES, CLASSES], f32)
        last_bits = sb("last_bits", [NODES, CLASSES, NODES], f32)
        newest = sb("newest", [NODES, NODES], f32)
        newest_c = sb("newest_c", [NODES, NODES], f32)
        mask = sb("mask", [NODES, NODES], f32)
        neg_max = sb("neg_max", [NODES, HEADS], f32)
        exp_sum = sb("exp_sum", [NODES, HEADS], f32)
        exp_inv = sb("exp_inv", [NODES, HEADS], f32)
        stats = sb("stats", [NODES, 2, HALVES, 6], f32)
        moments = sb("moments", [NODES, 2, 2], f32)
        std = sb("std", [NODES, 2], f32)
        rstd = sb("rstd", [NODES, 2], f32)
        eps = sb("eps", [NODES, 1], f32)

        psum = ctx.enter_context(nc.psum_tensor("psum", [P, 8, BANK], f32))
        ACC = [0, 2]
        TR = 4
        U = 4
        X1_T = 2
        SCORE_BANKS = [2, 3, 7, 6]
        PV_BANKS = [4, 5, 2, 3]
        DEGREE_BANKS = [7, 6]
        MEAN_BANKS = [(6, 7), (2, 3)]

        def span(t):
            return psum[:, t:t + 2, 0:SPAN // 2]

        raw_in = [sem(f"raw_in{n}") for n in range(RAW_SLOTS)]
        split_free = sem("split_free")
        high_ready = sem("high_ready")
        low_ready = sem("low_ready")
        full_ready = sem("full_ready")
        high_op_ready = sem("high_op_ready")
        op_ready = [sem(f"op_ready{s}") for s in range(3)]
        natural_ready = sem("natural_ready")
        transposed = sem("transposed")
        xT_in, pair_in, edges_in = sem("xT_in"), sem("pair_in"), sem("edges_in")
        kinds_in, biases_in, x_in, rows_in = sem("kinds_in"), sem("biases_in"), sem("x_in"), sem("rows_in")
        consts = sem("consts")
        pair_ready = sem("pair_ready")
        edge_f_ready, edges_T, edges_copied = sem("edge_f_ready"), sem("edges_T"), sem("edges_copied")
        keys_ready = sem("keys_ready")
        keys_used = sem("keys_used")
        hot_ready = sem("hot_ready")
        bits_ready, bits_copied = sem("bits_ready"), sem("bits_copied")
        kind_a, kind_e, kind_l = sem("kind_a"), sem("kind_e"), sem("kind_l")
        scores_ready = sem("scores_ready")
        max_ready = sem("max_ready")
        exp_ready = sem("exp_ready")
        probs_ready = sem("probs_ready")
        probs_T_ready = sem("probs_T_ready")
        probs_T_copied = sem("probs_T_copied")
        v2_ready = sem("v2_ready")
        pv_ready = sem("pv_ready")
        counts_packed, counts_ready = sem("counts_packed"), sem("counts_ready")
        degree_ready, degree_copied = sem("degree_ready"), sem("degree_copied")
        adj_ready, adj_high_ready, adj_low_ready = sem("adj_ready"), sem("adj_high_ready"), sem("adj_low_ready")
        resid_ready = sem("resid_ready")
        var_ready, std_ready = sem("var_ready"), sem("std_ready")
        x1_ready, x1_high_ready, x1_low_ready = sem("x1_ready"), sem("x1_high_ready"), sem("x1_low_ready")
        mean_sum = sem("mean_sum")
        mean_out = [sem("mean_out_scalar"), sem("mean_out_vector")]
        tanh_ready = sem("tanh_ready")
        z_ready = sem("z_ready")
        out_ready = sem("out_ready")
        out_done = sem("out_done")
        dve_step = sem("dve_step")

        X_OP = 2
        HALF_COLS = [slice(half * BANK, (half + 1) * BANK) for half in range(HALVES)]

        def arrivals(matrix):
            return 16 * (matrix // 2 + 1)

        def used(matrix):
            return SPLIT_SLOTS + splits_before(matrix + 1)

        def split_chunks(matrix):
            todo = [c for c in range(CHUNKS) if c not in plain_chunks(matrix)]
            return [(n, c, matrix % 2 * QUARTERS + c // CHUNKS_PER_QUARTER, c % CHUNKS_PER_QUARTER * FEATURES,
                     (splits_before(matrix) + n) % SPLIT_SLOTS) for n, c in enumerate(todo)]

        block = ctx.enter_context(nc.Block())

        @block.sync
        def _(sp):
            sp.dma_start(full_op[X_OP][:, :], xT).then_inc(xT_in, 16)
            for slot in range(RAW_SLOTS):
                sp.dma_start(raw[:, slot, :], weights[slot, :, :]).then_inc(raw_in[slot], 16)

            def load_pair(before, trip, step):
                for slot in range(RAW_SLOTS):
                    parity, quarter = divmod(slot, QUARTERS)
                    matrix, last = before + parity, quarter * CHUNKS_PER_QUARTER + CHUNKS_PER_QUARTER - 1
                    made = splits_before(matrix) + sum(c not in plain_chunks(matrix) for c in range(last + 1))
                    if any(c // CHUNKS_PER_QUARTER == quarter for c in plain_chunks(matrix)):
                        sp.wait_ge(split_free, trip * step + (SPLIT_SLOTS + made))
                    else:
                        sp.wait_ge(low_ready, trip * step + made)
                    src = weights[(before + 2) * QUARTERS + slot:, :, :][bass.ds(trip * RAW_SLOTS, 1), :, :]
                    sp.dma_start(raw[:, slot, :], src.rearrange("a p n -> (a p) n")).then_inc(raw_in[slot], 16)

            with sp.Fori(0, 3) as trip:
                load_pair(K, trip, 2 * splits(K))
            load_pair(OUT, 0, 0)
            with sp.Fori(0, 4) as trip:
                load_pair(ROOT, trip, 2 * splits(ROOT))
            for half in range(HALVES):
                sp.wait_ge(out_ready, half + 1)
                sp.dma_start(out[:, HALF_COLS[half]], resid[:, HALF_COLS[half]]).then_inc(out_done, 16)
            sp.wait_ge(out_done, 16 * HALVES)

        @block.gpsimd
        def _(pool):
            nc.gpsimd.memset(ident[:, :], 0.0).then_inc(split_free, SPLIT_SLOTS)
            nc.gpsimd.memset(not_later[:, :, :], BIG_KEY).then_inc(consts, 1)
            pool.wait_ge(consts, 1)
            nc.gpsimd.affine_select(out=ident[:, :], in_=ident[:, :], compare_op=ALU.not_equal, fill=1.0,
                                    base=0, pattern=[[-1, P]], channel_multiplier=1).then_inc(consts, 1)
            nc.gpsimd.affine_select(out=not_later[:, :, :], in_=not_later[:, :, :], compare_op=ALU.is_ge,
                                    fill=0.0, base=0, pattern=[[0, 4], [-1, P]],
                                    channel_multiplier=1).then_inc(consts, 1)
            nc.gpsimd.iota(key_w[:, :], [[0, P]], base=NODES, channel_multiplier=1 - NODES,
                           allow_small_or_imprecise_dtypes=True)
            nc.gpsimd.iota(neg_key_w[:, :], [[0, P]], base=-NODES, channel_multiplier=NODES - 1,
                           allow_small_or_imprecise_dtypes=True)
            pool.wait_ge(consts, 3)
            nc.gpsimd.tensor_copy(ident_b[:, :], ident[:, :]).then_inc(consts, 1)
            nc.gpsimd.iota(index[:, :], [[1, CLASSES * NODES]], base=0, channel_multiplier=0,
                           allow_small_or_imprecise_dtypes=True)
            nc.gpsimd.iota(powers[:, :], [[P, EDGE_CHUNKS]], base=127 * P, channel_multiplier=0,
                           allow_small_or_imprecise_dtypes=True)
            nc.gpsimd.memset(ones[:, :], 1.0)
            nc.gpsimd.memset(ones_r[:, :].bitcast(f32), 1.0)
            nc.gpsimd.memset(eps[:, :], EPS).then_inc(consts, 1)

        CONST_IDENT, CONST_KEYS, CONST_ALL = 3, 4, 5

        @block.scalar
        def _(act):
            act.dma_start(pair_i, edge_pair).then_inc(pair_in, 16)
            act.dma_start(edge_i[:, :], edge_rows).then_inc(edges_in, 16)
            act.dma_start(kind[:, :], type_weights).then_inc(kinds_in, 16)
            act.dma_start(biases[:, :, :], bias_T).then_inc(biases_in, 16)
            act.dma_start(resid[:, :], x).then_inc(x_in, 16)
            for r in range(3):
                act.dma_start(rows[32 * r:32 * r + 1, :], bias_rows[r:r + 1, :]).then_inc(rows_in, 16)

            def split_high(matrix, ns, trip=None):
                for n, chunk, slot, at, ring in [x for x in split_chunks(matrix) if x[0] in ns]:
                    loads, taken = arrivals(matrix), splits_before(matrix) + n + 1
                    if trip is not None:
                        loads, taken = trip * 16 + loads, trip * (2 * CHUNKS) + taken
                    act.wait_ge(raw_in[slot], loads)
                    act.wait_ge(split_free, taken)
                    nc.scalar.copy(high[:, ring, :], raw[:, slot, at:at + FEATURES]).then_inc(high_ready, 1)

            def copy_natural(matrix, bank, before):
                act.wait_ge(split_free, used(matrix))
                if before:
                    act.wait_ge(transposed, before)
                nc.scalar.copy(natural[:, :].rearrange("n (b f) -> n b f", b=HALVES),
                               psum[0:NODES, bank:bank + 2, :]).then_inc(natural_ready, 1)

            def high_operand(s, n):
                act.wait_ge(full_ready, n)
                nc.scalar.copy(high_op[s][:, :], full_op[s][:, :]).then_inc(high_op_ready, 1)

            def high_from_psum(s, n):
                act.wait_ge(transposed, n)
                nc.scalar.copy(high_op[s][:, :].rearrange("p (b n) -> p b n", b=2),
                               span(X1_T)).then_inc(high_op_ready, 1)

            act.wait_ge(xT_in, 16)
            nc.scalar.copy(high_op[X_OP][:, :], full_op[X_OP][:, :]).then_inc(high_op_ready, 1)
            act.wait_ge(pair_in, 16)
            nc.scalar.copy(pair_b, pair_i).then_inc(pair_ready, 1)
            split_high(K, range(3))
            act.wait_ge(kind_a, 1)
            nc.scalar.activation(kind_exp[:, :], kind_abs[:, :], ACT.Exp, scale=-1.0).then_inc(kind_e, 1)
            act.wait_ge(kind_e, 1)
            act.wait_ge(consts, CONST_ALL)
            nc.scalar.activation(kind_log[:, :], kind_exp[:, :], ACT.Ln,
                                 bias=ones[0:NODES, 0:1]).then_inc(kind_l, 1)
            split_high(K, range(3, 6))

            for matrix, product, bank, s in ((Q, K, 0, 0), (K2, Q, 2, 1), (Q2, K2, 0, None), (V, Q2, 2, None)):
                split_high(matrix, range(3))
                copy_natural(product, bank, product)
                split_high(matrix, range(3, 5))
                if s is not None:
                    high_operand(s, product + 1)
                if matrix == V:
                    act.wait_ge(bits_ready, 1)
                    nc.scalar.copy(last_bits[:, :, :], psum[0:NODES, 6, 0:GROUP].rearrange(
                        "s (k d) -> s k d", k=CLASSES)).then_inc(bits_copied, 1)
                split_high(matrix, range(5, 6))
            split_high(V2, range(3))
            copy_natural(V, 0, 4)
            split_high(V2, range(3, 4))
            high_operand(X_OP, 5)

            def exponentials(group):
                act.wait_ge(max_ready, group + 1)
                for h in range(group * HEADS_PER_GROUP, (group + 1) * HEADS_PER_GROUP):
                    cols = slice(h * NODES, (h + 1) * NODES)
                    last = nc.scalar.activation(probs[:, cols], probs[:, cols], ACT.Exp,
                                                bias=neg_max[:, h:h + 1], accum_out=exp_sum[:, h:h + 1])
                last.then_inc(exp_ready, 1)

            exponentials(0)
            exponentials(1)
            split_high(V2, range(4, 5))
            exponentials(2)
            exponentials(3)
            split_high(V2, range(5, 6))
            nc.scalar.preload_act_table(ACT.Sqrt)
            split_high(OUT, range(2))
            for group in (1, 3):
                act.wait_ge(probs_T_ready, group + 1)
                nc.scalar.copy(probs_T[:, group * GROUP:(group + 1) * GROUP],
                               psum[0:NODES, SCORE_BANKS[group], 0:GROUP]).then_inc(probs_T_copied, 1)
            act.wait_ge(split_free, used(V2))
            nc.scalar.copy(v2.rearrange("n (b f) -> n b f", b=HALVES),
                           psum[0:NODES, 0:2, :]).then_inc(v2_ready, 1)
            split_high(OUT, range(2, 4))
            high_operand(0, 6)
            act.wait_ge(adj_ready, 1)
            nc.scalar.copy(adj_high[:, :], adj).then_inc(adj_high_ready, 1)
            split_high(OUT, range(4, 6))
            split_high(GATE_X, range(3))
            act.wait_ge(var_ready, 1)
            nc.scalar.activation(std[:, 0:1], moments[:, 0, 1:2], ACT.Sqrt, bias=eps[:, :]).then_inc(std_ready, 1)
            for half, cols in enumerate(HALF_COLS):
                act.wait_ge(x1_ready, half + 1)
                nc.scalar.copy(x1_high[:, cols], x1[:, cols]).then_inc(x1_high_ready, 1)
            high_from_psum(1, 6)
            split_high(GATE_X, range(3, 4))
            means_v = means.rearrange("p (r k d) -> p r k d", r=RELATIONS, k=CHUNKS)
            for k in range(CHUNKS):
                act.wait_ge(mean_sum, k + 1)
                nc.scalar.copy(means_v[:, 0:4, k, :], psum[:, MEAN_BANKS[k % 2][0], 0:GROUP].rearrange(
                    "p (r d) -> p r d", r=4)).then_inc(mean_out[0], 1)
            split_high(GATE_X, range(4, 8))
            split_high(ROOT, range(CHUNKS))

            def mean_operand(s, relation, free):
                act.wait_ge(split_free, free)
                nc.scalar.copy(high_op[s][:, :], means[:, bass.ds(relation * SPAN, SPAN)]).then_inc(high_op_ready, 1)

            act.wait_ge(mean_out[1], CHUNKS)
            act.wait_ge(mean_out[0], CHUNKS)
            with act.Fori(0, RELATIONS // 2) as trip:
                mean_operand(0, trip * 2, trip * (2 * CHUNKS) + used(REL0 - 2))
                split_high(REL0, range(CHUNKS), trip)
                mean_operand(1, trip * 2 + 1, trip * (2 * CHUNKS) + used(REL0 - 1))
                split_high(REL0 + 1, range(CHUNKS), trip)
            split_high(GATE_U, range(3))
            copy_natural(GATE_U - 1, U, 6)
            split_high(GATE_U, range(3, 4))
            high_from_psum(0, 7)
            nc.scalar.activation(tanh_u.rearrange("n (b f) -> n b f", b=HALVES), psum[0:NODES, U:U + 2, :],
                                 ACT.Tanh).then_inc(tanh_ready, 1)
            split_high(GATE_U, range(4, CHUNKS))
            nc.scalar.preload_act_table(ACT.Sqrt)
            act.wait_ge(var_ready, 2)
            nc.scalar.activation(std[:, 1:2], moments[:, 1, 1:2], ACT.Sqrt, bias=eps[:, :]).then_inc(std_ready, 1)

        @block.vector
        def _(dve):
            steps = [0]

            def step(instruction):
                steps[0] += 1
                instruction.then_inc(dve_step, 1)

            def split_low(matrix, ns, trip=None):
                for n, chunk, slot, at, ring in [x for x in split_chunks(matrix) if x[0] in ns]:
                    made = splits_before(matrix) + n + 1
                    if trip is not None:
                        made = trip * (2 * CHUNKS) + made
                    dve.wait_ge(high_ready, made)
                    nc.vector.tensor_tensor(low[:, ring, :], raw[:, slot, at:at + FEATURES],
                                            high[:, ring, :].bitcast(f32), ALU.subtract).then_inc(low_ready, 1)

            def low_operand(s, n):
                dve.wait_ge(high_op_ready, n)
                nc.vector.tensor_tensor(low_op[s][:, :], full_op[s][:, :], high_op[s][:, :].bitcast(f32),
                                        ALU.subtract).then_inc(op_ready[s], 1)

            def low_from_psum(s, n):
                dve.wait_ge(high_op_ready, n)
                nc.vector.tensor_tensor(low_op[s][:, :].rearrange("p (b n) -> p b n", b=2), span(X1_T),
                                        high_op[s][:, :].bitcast(f32).rearrange("p (b n) -> p b n", b=2),
                                        ALU.subtract).then_inc(op_ready[s], 1)

            def biased_operand(s, n):
                dve.wait_ge(transposed, n + 1)
                nc.vector.tensor_tensor(
                    full_op[s][:, :].rearrange("p (b k d) -> p b k d", b=2, k=CHUNKS // 2),
                    span(TR).rearrange("p b (k d) -> p b k d", k=CHUNKS // 2),
                    biases[:, n, :].rearrange("p (b k) -> p b k", b=2).unsqueeze(3)
                    .broadcast_to([P, 2, CHUNKS // 2, NODES]), ALU.add).then_inc(full_ready, 1)

            low_operand(X_OP, 1)
            dve.wait_ge(edges_in, 16)
            nc.vector.tensor_copy(edge_f[:, :], edge_i[:, :]).then_inc(edge_f_ready, 1)
            dve.wait_ge(kinds_in, 16)
            nc.vector.scalar_tensor_tensor(kind_abs[:, :], kind[:, :], -1.0, kind[:, :],
                                           ALU.mult, ALU.max).then_inc(kind_a, 1)
            split_low(K, range(2))
            dve.wait_ge(edges_T, 1)
            nc.vector.tensor_copy(edge_c[:, :, :], psum[:, 6, 0:4 * EDGE_CHUNKS].rearrange(
                "p (a c) -> p a c", a=4)).then_inc(edges_copied, 1)
            split_low(K, range(2, 4))
            for bank in range(EDGE_CHUNKS // 4):
                dve.wait_ge(keys_ready, bank + 1)
                nc.vector.tensor_reduce(nearest[:, 4 * bank:4 * bank + 4],
                                        psum[:, bank + 2, :].rearrange("p (c j) -> p c j", c=4),
                                        axis=AX.X, op=ALU.min, apply_absolute_value=True).then_inc(keys_used, 1)
            split_low(K, range(4, 6))
            src_c, dst_c, type5_c, type8_c = (edge_c[:, n, :] for n in range(4))
            dve.wait_ge(consts, CONST_ALL)
            dve.wait_ge(edges_copied, 1)
            step(nc.vector.tensor_scalar(tmp_a[:, :], type5_c, 0.0, float(CLASSES * NODES), ALU.is_equal, ALU.mult))
            step(nc.vector.scalar_tensor_tensor(tmp_b[:, :], type5_c, float(NODES), dst_c, ALU.mult, ALU.add))
            step(nc.vector.tensor_scalar(count_at[:, :], type8_c, 4.0, None, ALU.is_ge))
            dve.wait_ge(keys_used, EDGE_CHUNKS // 4)
            step(nc.vector.scalar_tensor_tensor(mask_w[:, :], nearest[:, :], 0.0, powers[:, :].bitcast(bf16),
                                                ALU.is_gt, ALU.mult))
            dve.wait_ge(dve_step, steps[0])
            step(nc.vector.scalar_tensor_tensor(mask_at[:, :], tmp_b[:, :], -float(NODES), tmp_a[:, :],
                                                ALU.add, ALU.add))
            step(nc.vector.tensor_scalar(count_w[:, :], count_at[:, :], PACK - 1.0, 1.0, ALU.mult, ALU.add))
            dve.wait_ge(dve_step, steps[0])
            step(nc.vector.scalar_tensor_tensor(tmp_a[:, :], count_at[:, :], -4.0, type8_c, ALU.mult, ALU.add))
            dve.wait_ge(dve_step, steps[0])
            step(nc.vector.scalar_tensor_tensor(count_at[:, :], tmp_a[:, :], float(NODES), dst_c, ALU.mult, ALU.add))
            dve.wait_ge(kind_l, 1)
            step(nc.vector.scalar_tensor_tensor(kind_bias[:, :], kind[:, :], 0.0, kind_log[:, :], ALU.max, ALU.add))
            dve.wait_ge(dve_step, steps[0])
            dve.wait_ge(biases_in, 16)

            HOT_RUNS = 8
            def one_hots(run):
                per = EDGE_CHUNKS // HOT_RUNS
                with dve.Fori(0, per) as i:
                    chunk = i + run * per
                    def column(t):
                        return t[:, bass.ds(chunk, 1)]
                    nc.vector.tensor_scalar(src_hot[:, bass.ds(chunk * NODES, NODES)], index[:, 0:NODES],
                                            edge_c[:, 0, bass.ds(chunk, 1)], None, ALU.is_equal)
                    nc.vector.tensor_scalar(mask_hot[:, bass.ds(chunk * GROUP, GROUP)], index[:, :],
                                            column(mask_at), column(mask_w), ALU.is_equal, ALU.mult)
                    nc.vector.tensor_scalar(count_hot[:, bass.ds(chunk * GROUP, GROUP)], index[:, :],
                                            column(count_at), column(count_w), ALU.is_equal,
                                            ALU.mult).then_inc(hot_ready, 1)

            for matrix, product, s in ((Q, K, 0), (K2, Q, 1), (Q2, K2, 0), (V, Q2, 1)):
                split_low(matrix, range(2))
                if matrix == V:
                    one_hots(6)
                    one_hots(7)
                else:
                    one_hots(2 * product)
                split_low(matrix, range(2, 4))
                biased_operand(s, product)
                split_low(matrix, range(4, 5))
                if matrix in (Q, K2):
                    low_operand(s, product + 2)
                if matrix != V:
                    one_hots(2 * product + 1)
                split_low(matrix, range(5, 6))
            split_low(V2, range(3))

            dve.wait_ge(bits_copied, 1)
            step(nc.vector.scalar_tensor_tensor(last_bits[:, 3, :], ident[0:NODES, 0:NODES], 0.5,
                                                last_bits[:, 3, :], ALU.mult, ALU.max))
            dve.wait_ge(dve_step, steps[0])
            step(nc.vector.tensor_reduce(newest[:, :], last_bits[:, :, :].rearrange("s k d -> s d k"),
                                         axis=AX.X, op=ALU.max))
            dve.wait_ge(dve_step, steps[0])
            step(nc.vector.tensor_scalar(mask[:, :], newest[:, :], 0.0, NO_EDGE, ALU.is_equal, ALU.mult))
            step(nc.vector.tensor_scalar(newest_c[:, :], newest[:, :], 0.25, None, ALU.max))
            dve.wait_ge(dve_step, steps[0])
            step(nc.vector.tensor_tensor(last_bits[:, :, :], last_bits[:, :, :],
                                         newest_c[:, :].unsqueeze(1).broadcast_to([NODES, CLASSES, NODES]),
                                         ALU.is_equal))
            for k in range(CLASSES):
                dve.wait_ge(dve_step, steps[0])
                step(nc.vector.scalar_tensor_tensor(mask[:, :], last_bits[:, k, :], kind_bias[:, k:k + 1],
                                                    mask[:, :], ALU.mult, ALU.add))

            def head_view(group):
                return probs[:, group * GROUP:(group + 1) * GROUP].rearrange("n (h m) -> n h m", h=HEADS_PER_GROUP)

            def group_cols(t, group):
                return t[:, group * HEADS_PER_GROUP:(group + 1) * HEADS_PER_GROUP]

            def masked_scores(group):
                dve.wait_ge(scores_ready, group + 1)
                dve.wait_ge(dve_step, steps[0])
                step(nc.vector.scalar_tensor_tensor(
                    head_view(group),
                    psum[0:NODES, SCORE_BANKS[group], 0:GROUP].rearrange("n (h m) -> n h m", h=HEADS_PER_GROUP),
                    SCALE, mask[:, :].unsqueeze(1).broadcast_to([NODES, HEADS_PER_GROUP, NODES]),
                    ALU.mult, ALU.add))
                dve.wait_ge(dve_step, steps[0])
                nc.vector.tensor_reduce(group_cols(neg_max, group), head_view(group), axis=AX.X, op=ALU.max,
                                        negate=True).then_inc(max_ready, 1)

            def normalise(group):
                dve.wait_ge(exp_ready, group + 1)
                step(nc.vector.reciprocal(group_cols(exp_inv, group), group_cols(exp_sum, group)))
                dve.wait_ge(dve_step, steps[0])
                nc.vector.tensor_tensor(
                    head_view(group), head_view(group),
                    group_cols(exp_inv, group).unsqueeze(2).broadcast_to([NODES, HEADS_PER_GROUP, NODES]),
                    ALU.mult).then_inc(probs_ready, 1)

            masked_scores(0)
            biased_operand(X_OP, V)
            masked_scores(1)
            low_operand(X_OP, 4)
            masked_scores(2)
            split_low(V2, range(3, 4))
            masked_scores(3)
            normalise(0)
            split_low(V2, range(4, 5))
            normalise(1)
            normalise(2)
            split_low(V2, range(5, 6))
            normalise(3)
            split_low(OUT, range(2))
            for group in (0, 2):
                dve.wait_ge(probs_T_ready, group + 1)
                nc.vector.tensor_copy(probs_T[:, group * GROUP:(group + 1) * GROUP],
                                      psum[0:NODES, SCORE_BANKS[group], 0:GROUP]).then_inc(probs_T_copied, 1)
            counts_f = counts[:, :].bitcast(f32)
            dve.wait_ge(counts_packed, 1)
            packed = psum[0:NODES, 6, 0:GROUP]
            step(nc.vector.tensor_scalar(hi_count[:, :], packed, 1.0 / PACK, 0.375, ALU.mult, ALU.subtract))
            dve.wait_ge(dve_step, steps[0])
            step(nc.vector.tensor_scalar(counts[:, GROUP:2 * GROUP], hi_count[:, :], ROUND, ROUND, ALU.add, ALU.subtract))
            dve.wait_ge(dve_step, steps[0])
            nc.vector.scalar_tensor_tensor(counts[:, 0:GROUP], counts_f[:, GROUP:2 * GROUP], -PACK, packed,
                                           ALU.mult, ALU.add).then_inc(counts_ready, 1)
            for i in range(GROUPS):
                dve.wait_ge(pv_ready, i + 1)
                both = psum[:, PV_BANKS[i], 0:4 * NODES].rearrange("p (k h d) -> p k h d", k=2, h=2)
                into = full_op[0][:, :].rearrange("p (k d) -> p k d", k=CHUNKS)
                for h in range(2):
                    part = slice(h * HEAD_DIM, (h + 1) * HEAD_DIM)
                    last = nc.vector.tensor_tensor(
                        into[part, 2 * i:2 * i + 2, :], both[part, :, h, :],
                        biases[part, V2, 2 * i:2 * i + 2].unsqueeze(2).broadcast_to([HEAD_DIM, 2, NODES]), ALU.add)
            last.then_inc(full_ready, 1)
            split_low(OUT, range(2, 3))
            low_operand(0, 5)
            dve.wait_ge(degree_ready, 1)
            for half, bank in enumerate(DEGREE_BANKS):
                last = nc.vector.tensor_scalar(adj[:, half * GROUP:(half + 1) * GROUP], psum[0:NODES, bank, 0:GROUP],
                                               1.0, None, ALU.max)
            last.then_inc(degree_copied, 1)
            split_low(OUT, range(3, 4))
            dve.wait_ge(degree_copied, 1)
            dve.wait_ge(counts_ready, 1)
            step(nc.vector.reciprocal(adj, adj))
            dve.wait_ge(dve_step, steps[0])
            nc.vector.tensor_tensor(adj, adj, counts_f, ALU.mult).then_inc(adj_ready, 1)
            split_low(OUT, range(4, 6))
            dve.wait_ge(adj_high_ready, 1)
            nc.vector.tensor_tensor(adj_low[:, :], adj, adj_high[:, :].bitcast(f32),
                                    ALU.subtract).then_inc(adj_low_ready, 1)
            split_low(GATE_X, range(3))

            dve.wait_ge(x_in, 16)
            dve.wait_ge(split_free, used(OUT))
            for half, cols in enumerate(HALF_COLS):
                nc.vector.tensor_tensor(resid[:, cols], psum[0:NODES, half, :], resid[:, cols],
                                        ALU.add).then_inc(resid_ready, 1)
            for half, cols in enumerate(HALF_COLS):
                dve.wait_ge(resid_ready, half + 1)
                step(nc.vector.bn_stats(stats[:, 0, half, :], resid[:, cols]))
            dve.wait_ge(dve_step, steps[0])
            nc.vector.bn_aggr(moments[:, 0, :], stats[:, 0, :, :].rearrange("p b s -> p (b s)")).then_inc(var_ready, 1)
            dve.wait_ge(std_ready, 1)
            step(nc.vector.reciprocal(rstd[:, 0:1], std[:, 0:1]))
            dve.wait_ge(var_ready, 1)
            dve.wait_ge(dve_step, steps[0])
            for cols in HALF_COLS:
                nc.vector.tensor_scalar(x1[:, cols], resid[:, cols], moments[:, 0, 0:1], rstd[:, 0:1],
                                        ALU.subtract, ALU.mult).then_inc(x1_ready, 1)
            for half, cols in enumerate(HALF_COLS):
                dve.wait_ge(x1_high_ready, half + 1)
                nc.vector.tensor_tensor(x1_low[:, cols], x1[:, cols], x1_high[:, cols].bitcast(f32),
                                        ALU.subtract).then_inc(x1_low_ready, 1)
            low_from_psum(1, 6)
            means_v = means.rearrange("p (r k d) -> p r k d", r=RELATIONS, k=CHUNKS)
            for k in range(CHUNKS):
                dve.wait_ge(mean_sum, k + 1)
                nc.vector.tensor_copy(means_v[:, 4:8, k, :], psum[:, MEAN_BANKS[k % 2][1], 0:GROUP].rearrange(
                    "p (r d) -> p r d", r=4)).then_inc(mean_out[1], 1)
                if k == 1:
                    split_low(GATE_X, range(3, 4))
            split_low(GATE_X, range(4, CHUNKS))
            nc.vector.tensor_scalar(twice_x1, x1[:, :], 2.0, None, ALU.mult)
            split_low(ROOT, range(CHUNKS))

            def mean_low_operand(s, relation, n):
                dve.wait_ge(high_op_ready, n)
                nc.vector.tensor_tensor(low_op[s][:, :], means[:, bass.ds(relation * SPAN, SPAN)],
                                        high_op[s][:, :].bitcast(f32), ALU.subtract).then_inc(op_ready[s], 1)

            dve.wait_ge(mean_out[0], CHUNKS)
            dve.wait_ge(mean_out[1], CHUNKS)
            with dve.Fori(0, RELATIONS // 2) as trip:
                mean_low_operand(0, trip * 2, trip * 2 + 7)
                split_low(REL0, range(CHUNKS), trip)
                mean_low_operand(1, trip * 2 + 1, trip * 2 + 8)
                split_low(REL0 + 1, range(CHUNKS), trip)
            split_low(GATE_U, range(4))
            low_from_psum(0, 15)
            split_low(GATE_U, range(4, 6))
            dve.wait_ge(tanh_ready, 1)
            step(nc.vector.tensor_tensor(tanh_less_x, tanh_u, x1[:, :], ALU.subtract))
            split_low(GATE_U, range(6, CHUNKS))
            for half, cols in enumerate(HALF_COLS):
                dve.wait_ge(dve_step, steps[0])
                dve.wait_ge(z_ready, half + 1)
                step(nc.vector.tensor_tensor(resid[:, cols], psum[0:NODES, half, :], tanh_less_x[:, cols], ALU.mult))
                dve.wait_ge(dve_step, steps[0])
                step(nc.vector.tensor_tensor(resid[:, cols], resid[:, cols], twice_x1[:, cols], ALU.add))
                dve.wait_ge(dve_step, steps[0])
                step(nc.vector.bn_stats(stats[:, 1, half, :], resid[:, cols]))
            dve.wait_ge(dve_step, steps[0])
            nc.vector.bn_aggr(moments[:, 1, :], stats[:, 1, :, :].rearrange("p b s -> p (b s)")).then_inc(var_ready, 1)
            dve.wait_ge(std_ready, 2)
            step(nc.vector.reciprocal(rstd[:, 1:2], std[:, 1:2]))
            dve.wait_ge(var_ready, 2)
            dve.wait_ge(dve_step, steps[0])
            for cols in HALF_COLS:
                nc.vector.tensor_scalar(resid[:, cols], resid[:, cols], moments[:, 1, 0:1], rstd[:, 1:2],
                                        ALU.subtract, ALU.mult).then_inc(out_ready, 1)

        @block.tensor
        def _(pe):
            def add(into, lhsT, rhs, start=False, stop=False):
                return nc.tensor.matmul(into, lhsT, rhs, start=start, stop=stop, skip_group_check=True)

            def product(matrix, s, acc, opened=False, ends=True, trip=None, between={}):
                split = {c: (n, ring) for n, c, _, _, ring in split_chunks(matrix)}
                for c in range(CHUNKS):
                    nodes = slice(c * NODES, (c + 1) * NODES)
                    first, final = c == 0 and not opened, c == CHUNKS - 1 and ends
                    if c not in split:
                        slot, k = matrix % 2 * QUARTERS + c // CHUNKS_PER_QUARTER, c % CHUNKS_PER_QUARTER
                        pe.wait_ge(raw_in[slot], arrivals(matrix))
                        for b in range(HALVES):
                            at = k * FEATURES + b * BANK
                            add(psum[0:NODES, acc + b, :], full_op[s][:, nodes], raw[:, slot, at:at + BANK],
                                start=first)
                    else:
                        n, ring = split[c]
                        made = splits_before(matrix) + n + 1
                        if trip is not None:
                            made = trip * (2 * CHUNKS) + made
                        pe.wait_ge(low_ready, made)
                        for b in range(HALVES):
                            for lhsT, rhs in ((high_op, high), (low_op, high), (high_op, low)):
                                last = add(psum[0:NODES, acc + b, :], lhsT[s][:, nodes],
                                           rhs[:, ring, b * BANK:(b + 1) * BANK],
                                           start=first and lhsT is high_op and rhs is high,
                                           stop=final and rhs is low)
                            if matrix == GATE_U and final and b == 0:
                                last.then_inc(z_ready, 1)
                        last.then_inc(z_ready if matrix == GATE_U and final else split_free, 1)
                    if c in between:
                        between[c]()

            def transposes(bank, source, ks=range(CHUNKS)):
                for k in ks:
                    b, at = divmod(k, CHUNKS // 2)
                    last = nc.tensor.transpose(psum[:, bank + b, at * NODES:(at + 1) * NODES],
                                               source[:, k * P:(k + 1) * P], ident[0:NODES, 0:NODES])
                return last

            def transpose_product(n):
                pe.wait_ge(natural_ready, n + 1)
                if n:
                    pe.wait_ge(full_ready, n)
                transposes(TR, natural).then_inc(transposed, 1)

            def open_with_bias(acc, row):
                at = 32 * row
                for b in range(HALVES):
                    add(psum[0:NODES, acc + b, :], ones[at:at + 1, 0:NODES],
                        rows[at:at + 1, b * BANK:(b + 1) * BANK], start=True)

            def transpose_edges():
                pe.wait_ge(consts, CONST_IDENT)
                pe.wait_ge(edge_f_ready, 1)
                nc.tensor.transpose(psum[:, 6, 0:4 * EDGE_CHUNKS], edge_f[:, :],
                                    ident[0:4 * EDGE_CHUNKS, 0:4 * EDGE_CHUNKS]).then_inc(edges_T, 1)

            def key_differences():
                pe.wait_ge(consts, CONST_KEYS)
                pe.wait_ge(pair_ready, 1)
                pe.wait_ge(edges_copied, 1)
                for bank in range(EDGE_CHUNKS // 4):
                    into = psum[:, bank + 2, :]
                    add(into, key_w[:, :], pair_b[:, bank * BANK:(bank + 1) * BANK], start=True)
                    for j in range(4):
                        edges = slice(bank * BANK + j * P, bank * BANK + (j + 1) * P)
                        add(into[:, j * P:(j + 1) * P], pair_b[:, edges], neg_key_w[:, :])
                    add(into, ident_b[:, :], not_later[:, :, :].rearrange("p c j -> p (c j)"),
                        stop=True).then_inc(keys_ready, 1)

            def mask_bits():
                pe.wait_ge(hot_ready, EDGE_CHUNKS)
                for c in range(EDGE_CHUNKS):
                    last = add(psum[0:NODES, 6, 0:GROUP], src_hot[:, c * NODES:(c + 1) * NODES],
                               mask_hot[:, c * GROUP:(c + 1) * GROUP], start=c == 0, stop=c == EDGE_CHUNKS - 1)
                last.then_inc(bits_ready, 1)

            def scores(groups):
                for group in groups:
                    if SCORE_BANKS[group] == 6:
                        pe.wait_ge(bits_copied, 1)
                    part = slice(group % 2 * HEAD_DIM, (group % 2 + 1) * HEAD_DIM)
                    for j in range(HEADS_PER_GROUP):
                        chunk, at = group // 2 * HEADS_PER_GROUP + j, j * NODES
                        nodes = slice(chunk * NODES, (chunk + 1) * NODES)
                        last = add(psum[0:NODES, SCORE_BANKS[group], at:at + NODES], full_op[1][part, nodes],
                                   full_op[0][part, nodes], start=True, stop=True)
                    last.then_inc(scores_ready, 1)

            def transpose_probs(groups):
                for group in groups:
                    pe.wait_ge(probs_ready, group + 1)
                    for j in range(HEADS_PER_GROUP):
                        at = j * NODES
                        last = nc.tensor.transpose(psum[0:NODES, SCORE_BANKS[group], at:at + NODES],
                                                   probs[:, group * GROUP + at:group * GROUP + at + NODES],
                                                   ident[0:NODES, 0:NODES])
                    last.then_inc(probs_T_ready, 1)

            pe.wait_ge(op_ready[X_OP], 1)
            product(K, X_OP, 0, between={1: transpose_edges, 4: key_differences})
            pe.wait_ge(keys_used, EDGE_CHUNKS // 4)
            product(Q, X_OP, 2, between={2: lambda: transpose_product(K)})
            pe.wait_ge(op_ready[0], 1)
            product(K2, 0, 0, between={2: lambda: transpose_product(Q)})
            pe.wait_ge(op_ready[1], 1)
            product(Q2, 1, 2, between={2: lambda: transpose_product(K2)})
            product(V, X_OP, 0, between={2: lambda: transpose_product(Q2), 5: mask_bits})
            pe.wait_ge(full_ready, 4)
            scores([0, 1])
            transpose_product(V)
            scores([2, 3])
            pe.wait_ge(op_ready[X_OP], 2)
            product(V2, X_OP, 0, between={6: lambda: transpose_probs([0, 1]), 7: lambda: transpose_probs([2, 3])})
            pe.wait_ge(probs_T_copied, GROUPS)
            for c in range(EDGE_CHUNKS):
                last = add(psum[0:NODES, 6, 0:GROUP], src_hot[:, c * NODES:(c + 1) * NODES],
                           count_hot[:, c * GROUP:(c + 1) * GROUP], start=c == 0, stop=c == EDGE_CHUNKS - 1)
            last.then_inc(counts_packed, 1)
            pe.wait_ge(v2_ready, 1)
            by_chunk = probs_T.rearrange("m (u p k n) -> m u p k n", u=2, p=2, k=HEADS_PER_GROUP)
            for i in range(GROUPS):
                for k in range(2):
                    chunk = 2 * i + k
                    last = add(psum[:, PV_BANKS[i], k * 2 * NODES:(k + 1) * 2 * NODES],
                               v2[:, chunk * P:(chunk + 1) * P],
                               by_chunk[:, chunk // HEADS_PER_GROUP, :, chunk % HEADS_PER_GROUP, :],
                               start=True, stop=True)
                last.then_inc(pv_ready, 1)
            pe.wait_ge(rows_in, 48)
            pe.wait_ge(consts, CONST_ALL)
            open_with_bias(0, 0)
            pe.wait_ge(counts_ready, 1)
            for half, bank in enumerate(DEGREE_BANKS):
                last = add(psum[0:NODES, bank, 0:GROUP], ones_r[:, :], counts[:, half * GROUP:(half + 1) * GROUP],
                           start=True, stop=True)
            last.then_inc(degree_ready, 1)
            pe.wait_ge(op_ready[0], 2)
            product(OUT, 0, 0, opened=True)
            open_with_bias(U, 1)
            pe.wait_ge(resid_ready, HALVES)
            open_with_bias(0, 2)
            pe.wait_ge(adj_low_ready, 1)
            pe.wait_ge(x1_ready, 1)
            transposes(X1_T, x1, range(CHUNKS // 2))
            pe.wait_ge(x1_ready, 2)
            transposes(X1_T, x1, range(CHUNKS // 2, CHUNKS)).then_inc(transposed, 1)
            for k in range(CHUNKS):
                pe.wait_ge(x1_low_ready, 1 + k // (CHUNKS // 2))
                if k == 1:
                    pe.wait_ge(op_ready[1], 2)
                if k >= 2:
                    pe.wait_ge(mean_out[0], k - 1)
                    pe.wait_ge(mean_out[1], k - 1)
                for half in range(2):
                    cols = slice(half * GROUP, (half + 1) * GROUP)
                    into = psum[:, MEAN_BANKS[k % 2][half], 0:GROUP]
                    chunk = slice(k * P, (k + 1) * P)
                    add(into, x1_high[:, chunk], adj_high[:, cols], start=True)
                    add(into, x1_low[:, chunk], adj_high[:, cols])
                    last = add(into, x1_high[:, chunk], adj_low[:, cols], stop=True)
                last.then_inc(mean_sum, 1)
            pe.wait_ge(op_ready[1], 2)
            product(GATE_X, 1, 0, opened=True, ends=False)
            product(ROOT, 1, U, opened=True, ends=False)
            with pe.Fori(0, RELATIONS // 2) as trip:
                pe.wait_ge(op_ready[0], trip + 3)
                product(REL0, 0, U, opened=True, trip=trip)
                pe.wait_ge(op_ready[1], trip + 3)
                product(REL0 + 1, 1, U, opened=True, trip=trip)
            pe.wait_ge(mean_out[0], CHUNKS)
            pe.wait_ge(mean_out[1], CHUNKS)
            pe.wait_ge(natural_ready, 6)
            transposes(X1_T, natural).then_inc(transposed, 1)
            pe.wait_ge(op_ready[0], 7)
            product(GATE_U, 0, 0, opened=True)


def kernel(x, src, dst, edge_type_5, edge_type_8, L0_gnn_edge_type_weights, L0_gnn_wq, L0_gnn_bq, L0_gnn_wk,
           L0_gnn_bk, L0_gnn_wv, L0_gnn_bv, L0_gnn_wiq, L0_gnn_biq, L0_gnn_wik, L0_gnn_bik, L0_gnn_wiv,
           L0_gnn_biv, L0_gnn_wo, L0_gnn_bo, L1_gnn_weight, L1_gnn_root, L1_gnn_bias, L1_gnn_w_gate,
           L1_gnn_b_gate):
    import numpy as np
    import concourse.bacc as bacc
    from concourse import mybir as _mybir
    from concourse.bass_utils import run_bass_kernel_spmd

    def quarters(w):
        return w.reshape(QUARTERS, CHUNKS_PER_QUARTER, P, FEATURES).transpose(0, 2, 1, 3).reshape(
            QUARTERS, P, QUARTER)

    x, src, dst, type5, type8 = (np.asarray(a) for a in (x, src, dst, edge_type_5, edge_type_8))
    w_gate, relations = np.asarray(L1_gnn_w_gate), np.asarray(L1_gnn_weight)
    attention = [np.asarray(w).T for w in (L0_gnn_wk, L0_gnn_wq, L0_gnn_wik, L0_gnn_wiq, L0_gnn_wv, L0_gnn_wiv,
                                           L0_gnn_wo)]
    stream = attention + [w_gate[FEATURES:], np.asarray(L1_gnn_root)] + list(relations) + [w_gate[:FEATURES]]
    biases = [np.asarray(b).reshape(CHUNKS, P).T for b in (L0_gnn_bk, L0_gnn_bq, L0_gnn_bik, L0_gnn_biq,
                                                           L0_gnn_bv, L0_gnn_biv)]
    arrays = {
        "weights": np.concatenate([quarters(w) for w in stream]),
        "xT": x.reshape(NODES, CHUNKS, P).transpose(2, 1, 0).reshape(P, SPAN),
        "x": x,
        "edge_rows": np.concatenate([a.reshape(EDGE_CHUNKS, P) for a in (src, dst, type5, type8)]),
        "edge_pair": np.stack([src, dst]),
        "type_weights": np.broadcast_to(np.asarray(L0_gnn_edge_type_weights), (NODES, CLASSES)),
        "bias_T": np.stack(biases, axis=1),
        "bias_rows": np.stack([np.asarray(b) for b in (L0_gnn_bo, L1_gnn_bias, L1_gnn_b_gate)]),
    }
    nc = bacc.Bacc("TRN2", target_bir_lowering=False, num_devices=1)
    given, args = {}, []
    for name, a in arrays.items():
        given[f"in_{name}"] = np.ascontiguousarray(a)
        args.append(nc.dram_tensor(f"in_{name}", a.shape, _mybir.dt.from_np(a.dtype), kind="ExternalInput").ap())
    out = nc.dram_tensor("out", (NODES, FEATURES), _mybir.dt.float32, kind="ExternalOutput").ap()
    gnn_block(nc, *args, out)
    r = run_bass_kernel_spmd(nc, [given], core_ids=[0])
    return r.results[0]["out"]
```

```python
from contextlib import ExitStack

import concourse.bass as bass
from concourse import mybir

NODES = 96
EDGES = 3072
FEATURES = 1024
HEADS = 16
HEAD_DIM = FEATURES // HEADS
RELATIONS = 8
CLASSES = 4
P = 128
CHUNKS = FEATURES // P
BANK = 512
HALVES = FEATURES // BANK
QUARTERS = 4
CHUNKS_PER_QUARTER = CHUNKS // QUARTERS
QUARTER = CHUNKS_PER_QUARTER * FEATURES
MATRICES = 18
RAW_SLOTS = 2 * QUARTERS
SPLIT_SLOTS = 4
PLAIN = (0, 4)
MIXED = 7
EDGE_CHUNKS = EDGES // P
SPAN = CHUNKS * NODES
K, Q, K2, Q2, V, V2, OUT, ROOT, REL0 = range(9)
GATE_X, GATE_U = MATRICES - 2, MATRICES - 1
HEADS_PER_GROUP = 4
GROUPS = HEADS // HEADS_PER_GROUP
NO_EDGE = -1.0e30
PACK = 4096.0
BIG_KEY = 16384.0
KIND_SHIFT = 21
KIND_BITS = (CLASSES - 1) << KIND_SHIFT
ROUND = 12582912.0
EPS = 1e-5


def plain_chunks(matrix):
    return PLAIN if matrix < MIXED else ()


def splits(matrix):
    return CHUNKS - len(plain_chunks(matrix))


def splits_before(matrix):
    return sum(splits(m) for m in range(matrix))


def gnn_block(nc, weights, xT, x, edge_rows, edge_pair, type_weights, bias_T, bias_rows, out):
    f32, f32r, bf16 = mybir.dt.float32, mybir.dt.float32r, mybir.dt.bfloat16
    i32, i16 = mybir.dt.int32, mybir.dt.int16
    ALU, ACT, AX = mybir.AluOpType, mybir.ActivationFunctionType, mybir.AxisListType
    SCALE = float(HEAD_DIM) ** -0.5
    GROUP = HEADS_PER_GROUP * NODES

    with ExitStack() as ctx:
        def sb(name, shape, dt):
            return ctx.enter_context(nc.sbuf_tensor(name, shape, dt))

        def sem(name):
            return ctx.enter_context(nc.semaphore(name))

        raw = sb("raw", [P, RAW_SLOTS, QUARTER], f32)
        high = sb("high", [P, SPLIT_SLOTS, FEATURES], f32r)
        low = sb("low", [P, SPLIT_SLOTS, FEATURES], f32r)
        full_op = [sb(f"full_op{s}", [P, SPAN], f32) for s in range(3)]
        high_op = [sb(f"high_op{s}", [P, SPAN], f32r) for s in range(3)]
        low_op = [sb(f"low_op{s}", [P, SPAN], f32r) for s in range(3)]
        area = sb("area", [P, 9984], f32)
        mask_hot = area[:, 0:1152].bitcast(bf16)
        count_hot = area[:, 4224:8832].bitcast(bf16)
        src_hot = area[:, 8832:9984].bitcast(bf16)
        pair_i = area[0:2, 4224:7296].bitcast(i32)
        pair_b = area[0:2, 7296:8832].bitcast(bf16)
        probs = area[0:NODES, 0:1536]
        probs_T = area[0:NODES, 1536:3072]
        v2 = area[0:NODES, 3072:4096]
        degree_diag = area[0:NODES, 0:768]
        means = area[:, 0:RELATIONS * SPAN]
        tanh_u = area[0:NODES, 6144:7168]
        tanh_less_x = area[0:NODES, 7168:8192]
        twice_x1 = area[0:NODES, 8192:9216]
        adj = area[0:NODES, 9216:9984]
        natural = sb("natural", [NODES, FEATURES], f32)
        resid = sb("resid", [NODES, FEATURES], f32)
        x1 = sb("x1", [NODES, FEATURES], f32)
        x1_high = sb("x1_high", [NODES, FEATURES], f32r)
        x1_low = sb("x1_low", [NODES, FEATURES], f32r)
        counts = sb("counts", [NODES, RELATIONS * NODES], f32r)
        adj_high = sb("adj_high", [NODES, RELATIONS * NODES], f32r)
        adj_low = sb("adj_low", [NODES, RELATIONS * NODES], f32r)
        hi_count = sb("hi_count", [NODES, GROUP], f32)
        rows = sb("rows", [65, FEATURES], f32)
        rows_high, rows_low = x1_high[0:65, :], x1_low[0:65, :]
        biases = sb("biases", [P, 6, CHUNKS], f32)
        ident = sb("ident", [P, P], f32)
        ident_b = sb("ident_b", [P, P], bf16)
        ones = sb("ones", [P, P], f32)
        ones_r = sb("ones_r", [NODES, NODES], f32r)
        not_later = sb("not_later", [P, 4, P], bf16)
        key_w = sb("key_w", [2, P], bf16)
        neg_key_w = sb("neg_key_w", [2, P], bf16)
        index = sb("index", [P, CLASSES * NODES], i16)
        powers = sb("powers", [P, EDGE_CHUNKS], i16)
        edge_i = sb("edge_i", [4 * EDGE_CHUNKS, P], i32)
        edge_f = sb("edge_f", [4 * EDGE_CHUNKS, P], f32)
        edge_c = sb("edge_c", [P, 4, EDGE_CHUNKS], f32)
        nearest = sb("nearest", [P, EDGE_CHUNKS], f32)
        mask_w = sb("mask_w", [P, EDGE_CHUNKS], f32)
        digit = sb("digit", [P, EDGE_CHUNKS], f32)
        count_at = sb("count_at", [P, EDGE_CHUNKS], f32)
        count_w = sb("count_w", [P, EDGE_CHUNKS], f32)
        tmp_a = sb("tmp_a", [P, EDGE_CHUNKS], f32)
        tmp_b = sb("tmp_b", [P, EDGE_CHUNKS], f32)
        kind = sb("kind", [NODES, CLASSES], f32)
        kind_abs = sb("kind_abs", [NODES, CLASSES], f32)
        kind_exp = sb("kind_exp", [NODES, CLASSES], f32)
        kind_log = sb("kind_log", [NODES, CLASSES], f32)
        kind_bias = sb("kind_bias", [NODES, CLASSES], f32)
        history = sb("history", [NODES, NODES], f32)
        last_kind = sb("last_kind", [NODES, NODES], i32)
        by_kind = sb("by_kind", [NODES, CLASSES, NODES], f32)
        bias_of = sb("bias_of", [NODES, NODES], f32)
        degree = sb("degree", [NODES, RELATIONS], f32)
        degree_inv = sb("degree_inv", [NODES, RELATIONS], f32)
        mask = sb("mask", [NODES, NODES], f32)
        neg_max = sb("neg_max", [NODES, HEADS], f32)
        exp_sum = sb("exp_sum", [NODES, HEADS], f32)
        exp_inv = sb("exp_inv", [NODES, HEADS], f32)
        stats = sb("stats", [NODES, HALVES, 6], f32)
        z_stats = sb("z_stats", [NODES, HALVES, 6], f32)
        moments = sb("moments", [NODES, 2, 2], f32)
        std = sb("std", [NODES, 2], f32)
        rstd = sb("rstd", [NODES, 2], f32)
        shift = sb("shift", [NODES, 1], f32)
        eps = sb("eps", [NODES, 1], f32)

        psum = ctx.enter_context(nc.psum_tensor("psum", [P, 8, BANK], f32))
        TR = 4
        U = 4
        X1_T = 2
        SCORE_BANKS = [6, 2, 3, 7]
        PV_BANKS = [4, 5, 2, 3]
        KEY_BANKS = [2, 3, 4, 5, 7, 6]
        DEGREE_BANK = 7
        INVERSE_BANKS = [7, 6]
        MEAN_BANKS = [6, 2]

        def span(t):
            return psum[:, t:t + 2, 0:SPAN // 2]

        raw_in = [sem(f"raw_in{n}") for n in range(RAW_SLOTS)]
        split_free = sem("split_free")
        high_ready = sem("high_ready")
        low_ready = sem("low_ready")
        full_ready = sem("full_ready")
        high_op_ready = sem("high_op_ready")
        op_ready = [sem(f"op_ready{s}") for s in range(3)]
        natural_ready = sem("natural_ready")
        transposed = sem("transposed")
        xT_in, pair_in, edges_in = sem("xT_in"), sem("pair_in"), sem("edges_in")
        kinds_in, biases_in, x_in, rows_in = sem("kinds_in"), sem("biases_in"), sem("x_in"), sem("rows_in")
        consts = sem("consts")
        pair_ready = sem("pair_ready")
        edge_f_ready, edges_T, edges_copied = sem("edge_f_ready"), sem("edges_T"), sem("edges_copied")
        first_in = sem("first_in")
        v_natural = sem("v_natural")
        v_transposed, v_full, v_high = sem("v_transposed"), sem("v_full"), sem("v_high")
        attn_full, attn_high = sem("attn_full"), sem("attn_high")
        opened_ready = sem("opened_ready")
        rows_clear = sem("rows_clear")
        rows_high_ready, rows_low_ready = sem("rows_high_ready"), sem("rows_low_ready")
        keys_ready = sem("keys_ready")
        keys_used = sem("keys_used")
        src_hot_ready = sem("src_hot_ready")
        mask_hot_ready = sem("mask_hot_ready")
        count_hot_ready = sem("count_hot_ready")
        history_ready, history_read = sem("history_ready"), sem("history_read")
        kind_a, kind_e, kind_l = sem("kind_a"), sem("kind_e"), sem("kind_l")
        scores_ready = sem("scores_ready")
        max_ready = sem("max_ready")
        exp_ready = sem("exp_ready")
        probs_ready = sem("probs_ready")
        probs_T_ready = sem("probs_T_ready")
        probs_T_copied = sem("probs_T_copied")
        last_probs_T_copied = sem("last_probs_T_copied")
        v2_ready = sem("v2_ready")
        pv_ready = sem("pv_ready")
        counts_packed, counts_ready = sem("counts_packed"), sem("counts_ready")
        degree_ready, diag_ready, inverse_ready = sem("degree_ready"), sem("diag_ready"), sem("inverse_ready")
        adj_ready, adj_high_ready, adj_low_ready = sem("adj_ready"), sem("adj_high_ready"), sem("adj_low_ready")
        resid_ready = sem("resid_ready")
        var_ready, std_ready = sem("var_ready"), sem("std_ready")
        x1_ready, x1_high_ready, x1_low_ready = sem("x1_ready"), sem("x1_high_ready"), sem("x1_low_ready")
        mean_sum = sem("mean_sum")
        mean_out = sem("mean_out")
        tanh_ready = sem("tanh_ready")
        z_ready = sem("z_ready")
        shift_ready = sem("shift_ready")
        out_ready = [sem("out_ready_vector"), sem("out_ready_scalar")]
        out_done = sem("out_done")
        dve_step = sem("dve_step")

        X_OP = 2
        HALF_COLS = [slice(half * BANK, (half + 1) * BANK) for half in range(HALVES)]

        def arrivals(matrix):
            return 16 * (matrix // 2 + 1)

        def used(matrix):
            return SPLIT_SLOTS + splits_before(matrix + 1)

        def split_chunks(matrix):
            todo = [c for c in range(CHUNKS) if c not in plain_chunks(matrix)]
            return [(n, c, matrix % 2 * QUARTERS + c // CHUNKS_PER_QUARTER, c % CHUNKS_PER_QUARTER * FEATURES,
                     (splits_before(matrix) + n) % SPLIT_SLOTS) for n, c in enumerate(todo)]

        block = ctx.enter_context(nc.Block())

        @block.sync
        def _(sp):
            sp.dma_start(full_op[X_OP][:, :], xT).then_inc(xT_in, 16)
            sp.dma_start(raw[:, 0, 0:FEATURES], weights[0, :, 0:FEATURES]).then_inc(first_in, 16)
            sp.dma_start(raw[:, 0, FEATURES:QUARTER], weights[0, :, FEATURES:QUARTER]).then_inc(raw_in[0], 16)
            for slot in range(1, RAW_SLOTS):
                sp.dma_start(raw[:, slot, :], weights[slot, :, :]).then_inc(raw_in[slot], 16)
                if slot == 2:
                    sp.dma_start(biases[:, :, :], bias_T).then_inc(biases_in, 16)
            sp.dma_start(resid[:, :], x).then_inc(x_in, 16)
            sp.wait_ge(rows_clear, 1)
            for r in range(3):
                sp.dma_start(rows[32 * r:32 * r + 1, :], bias_rows[r:r + 1, :]).then_inc(rows_in, 16)

            def load_pair(before, trip, step):
                for slot in range(RAW_SLOTS):
                    parity, quarter = divmod(slot, QUARTERS)
                    matrix, last = before + parity, quarter * CHUNKS_PER_QUARTER + CHUNKS_PER_QUARTER - 1
                    made = splits_before(matrix) + sum(c not in plain_chunks(matrix) for c in range(last + 1))
                    if any(c // CHUNKS_PER_QUARTER == quarter for c in plain_chunks(matrix)):
                        sp.wait_ge(split_free, trip * step + (SPLIT_SLOTS + made))
                    else:
                        sp.wait_ge(low_ready, trip * step + made)
                    src = weights[(before + 2) * QUARTERS + slot:, :, :][bass.ds(trip * RAW_SLOTS, 1), :, :]
                    sp.dma_start(raw[:, slot, :], src.rearrange("a p n -> (a p) n")).then_inc(raw_in[slot], 16)

            with sp.Fori(0, 3) as trip:
                load_pair(K, trip, 2 * splits(K))
            load_pair(OUT, 0, 0)
            with sp.Fori(0, 4) as trip:
                load_pair(REL0, trip, 2 * splits(REL0))
            sp.wait_ge(out_ready[0], 1)
            sp.dma_start(out[:, HALF_COLS[0]], resid[:, HALF_COLS[0]]).then_inc(out_done, 16)
            sp.wait_ge(out_done, 16 * HALVES)

        @block.gpsimd
        def _(pool):
            nc.gpsimd.memset(ident[:, :], 0.0).then_inc(split_free, SPLIT_SLOTS)
            nc.gpsimd.memset(not_later[:, :, :], BIG_KEY).then_inc(consts, 1)
            pool.wait_ge(consts, 1)
            nc.gpsimd.affine_select(out=ident[:, :], in_=ident[:, :], compare_op=ALU.not_equal, fill=1.0,
                                    base=0, pattern=[[-1, P]], channel_multiplier=1).then_inc(consts, 1)
            nc.gpsimd.affine_select(out=not_later[:, :, :], in_=not_later[:, :, :], compare_op=ALU.is_ge,
                                    fill=0.0, base=0, pattern=[[0, 4], [-1, P]],
                                    channel_multiplier=1).then_inc(consts, 1)
            nc.gpsimd.iota(key_w[:, :], [[0, P]], base=NODES, channel_multiplier=1 - NODES,
                           allow_small_or_imprecise_dtypes=True)
            nc.gpsimd.iota(neg_key_w[:, :], [[0, P]], base=-NODES, channel_multiplier=NODES - 1,
                           allow_small_or_imprecise_dtypes=True)
            pool.wait_ge(consts, 3)
            nc.gpsimd.tensor_copy(ident_b[:, :], ident[:, :]).then_inc(consts, 1)
            nc.gpsimd.iota(index[:, :], [[1, CLASSES * NODES]], base=0, channel_multiplier=0,
                           allow_small_or_imprecise_dtypes=True)
            nc.gpsimd.iota(powers[:, :], [[4 * P, EDGE_CHUNKS]], base=127 * P, channel_multiplier=0,
                           allow_small_or_imprecise_dtypes=True)
            nc.gpsimd.memset(ones[:, :], 1.0)
            nc.gpsimd.memset(ones_r[:, :].bitcast(f32), 1.0)
            nc.gpsimd.memset(eps[:, :], EPS).then_inc(consts, 1)
            nc.gpsimd.memset(rows[:, :], 0.0).then_inc(rows_clear, 1)

        CONST_IDENT, CONST_KEYS, CONST_ALL = 3, 4, 5

        @block.scalar
        def _(act):
            act.dma_start(pair_i, edge_pair).then_inc(pair_in, 16)
            act.dma_start(edge_i[:, :], edge_rows).then_inc(edges_in, 16)
            act.dma_start(kind[:, :], type_weights).then_inc(kinds_in, 16)
            nc.scalar.preload_act_table(ACT.Exp)

            def split_high(matrix, ns, trip=None):
                for n, chunk, slot, at, ring in [x for x in split_chunks(matrix) if x[0] in ns]:
                    loads, taken = arrivals(matrix), splits_before(matrix) + n + 1
                    if trip is not None:
                        loads, taken = trip * 16 + loads, trip * (2 * CHUNKS) + taken
                    act.wait_ge(raw_in[slot], loads)
                    act.wait_ge(split_free, taken)
                    nc.scalar.copy(high[:, ring, :], raw[:, slot, at:at + FEATURES]).then_inc(high_ready, 1)

            def copy_natural(matrix, bank, before):
                act.wait_ge(split_free, used(matrix))
                if before:
                    act.wait_ge(transposed, before)
                nc.scalar.copy(natural[:, :].rearrange("n (b f) -> n b f", b=HALVES),
                               psum[0:NODES, bank:bank + 2, :]).then_inc(natural_ready, 1)

            def high_operand(s, n):
                act.wait_ge(full_ready, n)
                nc.scalar.copy(high_op[s][:, :], full_op[s][:, :]).then_inc(high_op_ready, 1)

            def high_from_psum(s, half, n):
                act.wait_ge(transposed, n)
                nc.scalar.copy(high_op[s][:, half * GROUP:(half + 1) * GROUP],
                               psum[:, X1_T + half, 0:GROUP]).then_inc(high_op_ready, 1)

            act.wait_ge(xT_in, 16)
            nc.scalar.copy(high_op[X_OP][:, :], full_op[X_OP][:, :]).then_inc(high_op_ready, 1)
            split_high(K, range(4))
            act.wait_ge(pair_in, 16)
            nc.scalar.copy(pair_b, pair_i).then_inc(pair_ready, 1)
            act.wait_ge(kind_a, 1)
            nc.scalar.activation(kind_exp[:, :], kind_abs[:, :], ACT.Exp, scale=-1.0).then_inc(kind_e, 1)
            act.wait_ge(kind_e, 1)
            act.wait_ge(consts, CONST_ALL)
            nc.scalar.activation(kind_log[:, :], kind_exp[:, :], ACT.Ln,
                                 bias=ones[0:NODES, 0:1]).then_inc(kind_l, 1)
            split_high(K, range(4, 6))

            for matrix, product, bank, s in ((Q, K, 0, 0), (K2, Q, 2, 1), (Q2, K2, 0, None)):
                split_high(matrix, range(3))
                copy_natural(product, bank, product)
                split_high(matrix, range(3, 5))
                if s is not None:
                    high_operand(s, product + 1)
                split_high(matrix, range(5, 6))

            def exponentials(group):
                act.wait_ge(max_ready, group + 1)
                for h in range(group * HEADS_PER_GROUP, (group + 1) * HEADS_PER_GROUP):
                    cols = slice(h * NODES, (h + 1) * NODES)
                    last = nc.scalar.activation(probs[:, cols], probs[:, cols], ACT.Exp,
                                                bias=neg_max[:, h:h + 1], accum_out=exp_sum[:, h:h + 1])
                last.then_inc(exp_ready, 1)

            def copy_probs_T(group):
                act.wait_ge(probs_T_ready, group + 1)
                nc.scalar.copy(probs_T[:, group * GROUP:(group + 1) * GROUP],
                               psum[0:NODES, SCORE_BANKS[group], 0:GROUP]).then_inc(probs_T_copied, 1)

            def high_half(s, half, full, made):
                cols = slice(half * GROUP, (half + 1) * GROUP)
                act.wait_ge(full, half + 1)
                nc.scalar.copy(high_op[s][:, cols], full_op[s][:, cols]).then_inc(made, 1)

            act.wait_ge(rows_in, 48)
            nc.scalar.copy(rows_high, rows[:, :]).then_inc(rows_high_ready, 1)
            split_high(V, range(3))
            copy_natural(Q2, 2, 3)
            split_high(V, range(3, 5))
            split_high(V, range(5, 6))
            exponentials(0)
            split_high(V2, range(1))
            act.wait_ge(split_free, used(V))
            act.wait_ge(transposed, 4)
            for half, cols in enumerate(HALF_COLS):
                nc.scalar.copy(natural[:, cols], psum[0:NODES, half, :]).then_inc(v_natural, 1)
            split_high(V2, range(1, 2))
            high_half(X_OP, 0, v_full, v_high)
            high_half(X_OP, 1, v_full, v_high)
            split_high(V2, range(2, 3))
            exponentials(1)
            split_high(V2, range(3, 4))
            exponentials(2)
            split_high(V2, range(4, 6))
            exponentials(3)
            copy_probs_T(0)
            copy_probs_T(1)
            split_high(OUT, range(1))
            copy_probs_T(2)
            act.wait_ge(split_free, used(V2))
            nc.scalar.copy(v2.rearrange("n (b f) -> n b f", b=HALVES),
                           psum[0:NODES, 0:2, :]).then_inc(v2_ready, 1)
            split_high(OUT, range(1, 3))
            high_half(0, 0, attn_full, attn_high)
            high_half(0, 1, attn_full, attn_high)
            split_high(OUT, range(3, 4))
            nc.scalar.preload_act_table(ACT.Sqrt)
            split_high(OUT, range(4, 6))
            split_high(ROOT, range(3))
            act.wait_ge(var_ready, 1)
            nc.scalar.activation(std[:, 0:1], moments[:, 0, 1:2], ACT.Sqrt, bias=eps[:, :]).then_inc(std_ready, 1)
            act.wait_ge(opened_ready, 3)
            for half, cols in enumerate(HALF_COLS):
                act.wait_ge(x1_ready, half + 1)
                nc.scalar.copy(x1_high[:, cols], x1[:, cols]).then_inc(x1_high_ready, 1)
            high_from_psum(X_OP, 0, 5)
            high_from_psum(X_OP, 1, 6)
            split_high(ROOT, range(3, 5))
            act.wait_ge(adj_ready, 1)
            nc.scalar.copy(adj_high[:, :], adj).then_inc(adj_high_ready, 1)
            split_high(ROOT, range(5, CHUNKS))
            means_v = means.rearrange("p (b r k d) -> p b r k d", b=2, r=RELATIONS // 2, k=CHUNKS)
            for k in range(CHUNKS):
                act.wait_ge(mean_sum, k + 1)
                nc.scalar.copy(means_v[:, :, :, k, :], span(MEAN_BANKS[k % 2]).rearrange(
                    "p b (r d) -> p b r d", r=RELATIONS // 2)).then_inc(mean_out, 1)

            def mean_operand(s, relation, free):
                act.wait_ge(mean_out, CHUNKS)
                act.wait_ge(split_free, free)
                nc.scalar.copy(high_op[s][:, :], means[:, bass.ds(relation * SPAN, SPAN)]).then_inc(high_op_ready, 1)

            with act.Fori(0, RELATIONS // 2) as trip:
                split_high(REL0, range(1), trip)
                mean_operand(0, trip * 2, trip * (2 * CHUNKS) + used(REL0 - 2))
                split_high(REL0, range(1, CHUNKS), trip)
                split_high(REL0 + 1, range(1), trip)
                mean_operand(1, trip * 2 + 1, trip * (2 * CHUNKS) + used(REL0 - 1))
                split_high(REL0 + 1, range(1, CHUNKS), trip)
            split_high(GATE_X, range(3))
            act.wait_ge(v_transposed, HALVES)
            copy_natural(GATE_X - 1, U, 0)
            split_high(GATE_X, range(3, 6))
            high_from_psum(0, 0, 7)
            split_high(GATE_X, range(6, 7))
            high_from_psum(0, 1, 7)
            split_high(GATE_X, range(7, CHUNKS))
            split_high(GATE_U, range(2))
            nc.scalar.preload_act_table(ACT.Tanh)
            split_high(GATE_U, range(2, CHUNKS))
            nc.scalar.activation(tanh_u.rearrange("n (b f) -> n b f", b=HALVES), psum[0:NODES, U:U + 2, :],
                                 ACT.Tanh).then_inc(tanh_ready, 1)
            nc.scalar.preload_act_table(ACT.Sqrt)
            act.wait_ge(var_ready, 2)
            nc.scalar.activation(std[:, 1:2], moments[:, 1, 1:2], ACT.Sqrt, bias=eps[:, :]).then_inc(std_ready, 1)
            act.wait_ge(shift_ready, 1)
            nc.scalar.activation(resid[:, HALF_COLS[1]], resid[:, HALF_COLS[1]], ACT.Identity,
                                 bias=shift[:, :], scale=rstd[:, 1:2]).then_inc(out_ready[1], 1)
            act.wait_ge(out_ready[1], 1)
            act.dma_start(out[:, HALF_COLS[1]], resid[:, HALF_COLS[1]]).then_inc(out_done, 16)

        @block.vector
        def _(dve):
            steps = [0]

            def step(instruction):
                steps[0] += 1
                instruction.then_inc(dve_step, 1)

            def split_low(matrix, ns, trip=None):
                for n, chunk, slot, at, ring in [x for x in split_chunks(matrix) if x[0] in ns]:
                    made = splits_before(matrix) + n + 1
                    if trip is not None:
                        made = trip * (2 * CHUNKS) + made
                    dve.wait_ge(high_ready, made)
                    nc.vector.tensor_tensor(low[:, ring, :], raw[:, slot, at:at + FEATURES],
                                            high[:, ring, :].bitcast(f32), ALU.subtract).then_inc(low_ready, 1)

            def low_operand(s, n):
                dve.wait_ge(high_op_ready, n)
                nc.vector.tensor_tensor(low_op[s][:, :], full_op[s][:, :], high_op[s][:, :].bitcast(f32),
                                        ALU.subtract).then_inc(op_ready[s], 1)

            def low_from_psum(s, half, n):
                cols = slice(half * GROUP, (half + 1) * GROUP)
                dve.wait_ge(high_op_ready, n)
                nc.vector.tensor_tensor(low_op[s][:, cols], psum[:, X1_T + half, 0:GROUP],
                                        high_op[s][:, cols].bitcast(f32), ALU.subtract).then_inc(op_ready[s], 1)

            def biased_operand(s, n):
                dve.wait_ge(transposed, n + 1)
                nc.vector.tensor_tensor(
                    full_op[s][:, :].rearrange("p (b k d) -> p b k d", b=2, k=CHUNKS // 2),
                    span(TR).rearrange("p b (k d) -> p b k d", k=CHUNKS // 2),
                    biases[:, n, :].rearrange("p (b k) -> p b k", b=2).unsqueeze(3)
                    .broadcast_to([P, 2, CHUNKS // 2, NODES]), ALU.add).then_inc(full_ready, 1)

            low_operand(X_OP, 1)
            dve.wait_ge(edges_in, 16)
            nc.vector.tensor_copy(edge_f[:, :], edge_i[:, :]).then_inc(edge_f_ready, 1)
            split_low(K, range(2))
            dve.wait_ge(kinds_in, 16)
            nc.vector.scalar_tensor_tensor(kind_abs[:, :], kind[:, :], -1.0, kind[:, :],
                                           ALU.mult, ALU.max).then_inc(kind_a, 1)
            dve.wait_ge(edges_T, 1)
            nc.vector.tensor_copy(edge_c[:, :, :], psum[:, 6, 0:4 * EDGE_CHUNKS].rearrange(
                "p (a c) -> p a c", a=4)).then_inc(edges_copied, 1)
            split_low(K, range(2, 4))
            src_c, dst_c, type5_c, type8_c = (edge_c[:, n, :] for n in range(4))
            dve.wait_ge(consts, CONST_ALL)
            dve.wait_ge(edges_copied, 1)
            step(nc.vector.tensor_scalar(tmp_a[:, :], type5_c, 0.0, float(CLASSES), ALU.is_equal, ALU.mult))
            step(nc.vector.tensor_scalar(count_at[:, :], type8_c, 4.0, None, ALU.is_ge))
            dve.wait_ge(dve_step, steps[0])
            step(nc.vector.scalar_tensor_tensor(tmp_b[:, :], type5_c, CLASSES - 1.0, tmp_a[:, :], ALU.add, ALU.add))
            step(nc.vector.tensor_scalar(count_w[:, :], count_at[:, :], PACK - 1.0, 1.0, ALU.mult, ALU.add))
            dve.wait_ge(dve_step, steps[0])
            step(nc.vector.tensor_tensor(digit[:, :], tmp_b[:, :], powers[:, :].bitcast(bf16), ALU.mult))
            step(nc.vector.scalar_tensor_tensor(tmp_a[:, :], count_at[:, :], -4.0, type8_c, ALU.mult, ALU.add))
            dve.wait_ge(dve_step, steps[0])
            step(nc.vector.scalar_tensor_tensor(count_at[:, :], tmp_a[:, :], float(NODES), dst_c, ALU.mult, ALU.add))

            def nearest_later(banks):
                for n in banks:
                    dve.wait_ge(keys_ready, n + 1)
                    nc.vector.tensor_reduce(nearest[:, 4 * n:4 * n + 4],
                                            psum[:, KEY_BANKS[n], :].rearrange("p (c j) -> p c j", c=4),
                                            axis=AX.X, op=ALU.min, apply_absolute_value=True).then_inc(keys_used, 1)

            def src_hots(chunks):
                n = len(chunks)
                last = nc.vector.tensor_tensor(
                    src_hot[:, chunks[0] * NODES:(chunks[-1] + 1) * NODES].rearrange("p (c s) -> p c s", c=n),
                    index[:, 0:NODES].unsqueeze(1).broadcast_to([P, n, NODES]),
                    edge_c[:, 0, chunks[0]:chunks[-1] + 1].unsqueeze(2).broadcast_to([P, n, NODES]), ALU.is_equal)
                last.then_inc(src_hot_ready, 1)

            src_hots(range(EDGE_CHUNKS // 2))
            split_low(K, range(4, 5))
            nearest_later(range(3))
            split_low(K, range(5, 6))
            split_low(Q, range(1))
            dve.wait_ge(kind_l, 1)
            step(nc.vector.scalar_tensor_tensor(kind_bias[:, :], kind[:, :], 0.0, kind_log[:, :], ALU.max, ALU.add))
            nearest_later(range(3, 6))
            dve.wait_ge(keys_used, EDGE_CHUNKS // 4)
            dve.wait_ge(dve_step, steps[0])
            step(nc.vector.scalar_tensor_tensor(mask_w[:, :], nearest[:, :], 0.0, digit[:, :], ALU.is_gt, ALU.mult))
            dve.wait_ge(dve_step, steps[0])
            dve.wait_ge(biases_in, 16)

            def column(t, chunk):
                return t[:, bass.ds(chunk, 1)]

            HOT_STEP = 6

            def mask_hots(first, count):
                with dve.Fori(0, count // HOT_STEP) as i:
                    for chunk in (i * HOT_STEP + (first + n) for n in range(HOT_STEP)):
                        nc.vector.tensor_scalar(mask_hot[:, bass.ds(chunk * NODES, NODES)], index[:, 0:NODES],
                                                edge_c[:, 1, bass.ds(chunk, 1)], column(mask_w, chunk),
                                                ALU.is_equal, ALU.mult).then_inc(mask_hot_ready, 1)

            def count_hots(first, count):
                with dve.Fori(0, count // HOT_STEP) as i:
                    for chunk in (i * HOT_STEP + (first + n) for n in range(HOT_STEP)):
                        nc.vector.tensor_scalar(count_hot[:, bass.ds(chunk * GROUP, GROUP)], index[:, :],
                                                column(count_at, chunk), column(count_w, chunk), ALU.is_equal,
                                                ALU.mult).then_inc(count_hot_ready, 1)

            split_low(Q, range(1, 2))
            src_hots(range(EDGE_CHUNKS // 2, EDGE_CHUNKS))
            split_low(Q, range(2, 4))
            biased_operand(0, K)
            split_low(Q, range(4, 5))
            low_operand(0, 2)
            mask_hots(0, 6)
            split_low(Q, range(5, 6))

            split_low(K2, range(2))
            mask_hots(6, 6)
            split_low(K2, range(2, 4))
            biased_operand(1, Q)
            split_low(K2, range(4, 5))
            low_operand(1, 3)
            split_low(K2, range(5, 6))

            split_low(Q2, range(2))
            mask_hots(12, 12)
            split_low(Q2, range(2, 4))
            biased_operand(0, K2)
            split_low(Q2, range(4, 5))
            split_low(Q2, range(5, 6))

            split_low(V, range(2))
            count_hots(0, 6)
            dve.wait_ge(rows_high_ready, 1)
            nc.vector.tensor_tensor(rows_low, rows[:, :], rows_high.bitcast(f32),
                                    ALU.subtract).then_inc(rows_low_ready, 1)
            dve.wait_ge(history_ready, 1)
            nc.vector.scalar_tensor_tensor(history[:, :], ident[0:NODES, 0:NODES], 7.0 / 16.0,
                                           psum[0:NODES, 6, 0:NODES], ALU.mult, ALU.max).then_inc(history_read, 1)
            dve.wait_ge(history_read, 1)
            step(nc.vector.tensor_scalar(mask[:, :], history[:, :], 0.0, NO_EDGE, ALU.is_equal, ALU.mult))
            step(nc.vector.tensor_scalar(last_kind[:, :], history[:, :].bitcast(i32), KIND_BITS, None,
                                         ALU.bitwise_and))
            dve.wait_ge(dve_step, steps[0])
            for k in range(CLASSES):
                step(nc.vector.tensor_scalar(by_kind[:, k, :], last_kind[:, :], float(k << KIND_SHIFT),
                                             kind_bias[:, k:k + 1], ALU.is_equal, ALU.mult))
            dve.wait_ge(dve_step, steps[0])
            step(nc.vector.tensor_reduce(bias_of[:, :], by_kind[:, :, :].rearrange("s k d -> s d k"),
                                         axis=AX.X, op=ALU.add))
            dve.wait_ge(dve_step, steps[0])
            step(nc.vector.tensor_tensor(mask[:, :], mask[:, :], bias_of[:, :], ALU.add))

            def head_view(group):
                return probs[:, group * GROUP:(group + 1) * GROUP].rearrange("n (h m) -> n h m", h=HEADS_PER_GROUP)

            def group_cols(t, group):
                return t[:, group * HEADS_PER_GROUP:(group + 1) * HEADS_PER_GROUP]

            def masked_scores(group):
                dve.wait_ge(scores_ready, group + 1)
                dve.wait_ge(dve_step, steps[0])
                step(nc.vector.scalar_tensor_tensor(
                    head_view(group),
                    psum[0:NODES, SCORE_BANKS[group], 0:GROUP].rearrange("n (h m) -> n h m", h=HEADS_PER_GROUP),
                    SCALE, mask[:, :].unsqueeze(1).broadcast_to([NODES, HEADS_PER_GROUP, NODES]),
                    ALU.mult, ALU.add))
                dve.wait_ge(dve_step, steps[0])
                nc.vector.tensor_reduce(group_cols(neg_max, group), head_view(group), axis=AX.X, op=ALU.max,
                                        negate=True).then_inc(max_ready, 1)

            def normalise(group):
                dve.wait_ge(exp_ready, group + 1)
                step(nc.vector.reciprocal(group_cols(exp_inv, group), group_cols(exp_sum, group)))
                dve.wait_ge(dve_step, steps[0])
                nc.vector.tensor_tensor(
                    head_view(group), head_view(group),
                    group_cols(exp_inv, group).unsqueeze(2).broadcast_to([NODES, HEADS_PER_GROUP, NODES]),
                    ALU.mult).then_inc(probs_ready, 1)

            def low_half(s, half, made):
                cols = slice(half * GROUP, (half + 1) * GROUP)
                dve.wait_ge(made, half + 1)
                nc.vector.tensor_tensor(low_op[s][:, cols], full_op[s][:, cols],
                                        high_op[s][:, cols].bitcast(f32), ALU.subtract).then_inc(op_ready[s], 1)

            split_low(V, range(2, 4))
            biased_operand(1, Q2)
            split_low(V, range(4, 5))
            count_hots(6, 6)
            masked_scores(0)
            split_low(V, range(5, 6))
            masked_scores(1)
            split_low(V2, range(1))
            normalise(0)
            for half in range(HALVES):
                dve.wait_ge(v_transposed, half + 1)
                nc.vector.tensor_tensor(
                    full_op[X_OP][:, half * GROUP:(half + 1) * GROUP].rearrange("p (k d) -> p k d", k=CHUNKS // 2),
                    psum[:, TR + half, 0:GROUP].rearrange("p (k d) -> p k d", k=CHUNKS // 2),
                    biases[:, V, half * CHUNKS // 2:(half + 1) * CHUNKS // 2].unsqueeze(2)
                    .broadcast_to([P, CHUNKS // 2, NODES]), ALU.add).then_inc(v_full, 1)
            split_low(V2, range(1, 2))
            low_half(X_OP, 0, v_high)
            low_half(X_OP, 1, v_high)
            split_low(V2, range(2, 3))
            masked_scores(2)
            split_low(V2, range(3, 4))
            masked_scores(3)
            split_low(V2, range(4, 5))
            normalise(1)
            split_low(V2, range(5, 6))
            normalise(2)
            normalise(3)
            count_hots(12, 6)
            dve.wait_ge(probs_T_ready, GROUPS)
            nc.vector.tensor_copy(probs_T[:, (GROUPS - 1) * GROUP:GROUPS * GROUP],
                                  psum[0:NODES, SCORE_BANKS[GROUPS - 1], 0:GROUP]).then_inc(last_probs_T_copied, 1)
            split_low(OUT, range(1))
            for i in range(GROUPS):
                dve.wait_ge(pv_ready, i + 1)
                both = psum[:, PV_BANKS[i], 0:4 * NODES].rearrange("p (k h d) -> p k h d", k=2, h=2)
                into = full_op[0][:, :].rearrange("p (k d) -> p k d", k=CHUNKS)
                for h in range(2):
                    part = slice(h * HEAD_DIM, (h + 1) * HEAD_DIM)
                    last = nc.vector.tensor_tensor(
                        into[part, 2 * i:2 * i + 2, :], both[part, :, h, :],
                        biases[part, V2, 2 * i:2 * i + 2].unsqueeze(2).broadcast_to([HEAD_DIM, 2, NODES]), ALU.add)
                if i % 2:
                    last.then_inc(attn_full, 1)
                if i == 2:
                    low_half(0, 0, attn_high)
                    split_low(OUT, range(1, 2))
            low_half(0, 1, attn_high)
            split_low(OUT, range(2, 4))
            count_hots(18, 6)
            split_low(OUT, range(4, 6))
            split_low(ROOT, range(2))

            dve.wait_ge(x_in, 16)
            dve.wait_ge(split_free, used(OUT))
            for half, cols in enumerate(HALF_COLS):
                nc.vector.tensor_tensor(resid[:, cols], psum[0:NODES, half, :], resid[:, cols],
                                        ALU.add).then_inc(resid_ready, 1)
            for half, cols in enumerate(HALF_COLS):
                dve.wait_ge(resid_ready, half + 1)
                step(nc.vector.bn_stats(stats[:, half, :], resid[:, cols]))
            dve.wait_ge(dve_step, steps[0])
            nc.vector.bn_aggr(moments[:, 0, :], stats[:, :, :].rearrange("p b s -> p (b s)")).then_inc(var_ready, 1)
            dve.wait_ge(std_ready, 1)
            step(nc.vector.reciprocal(rstd[:, 0:1], std[:, 0:1]))
            dve.wait_ge(var_ready, 1)
            dve.wait_ge(dve_step, steps[0])
            for cols in HALF_COLS:
                nc.vector.tensor_scalar(x1[:, cols], resid[:, cols], moments[:, 0, 0:1], rstd[:, 0:1],
                                        ALU.subtract, ALU.mult).then_inc(x1_ready, 1)
            low_from_psum(X_OP, 0, 4)
            low_from_psum(X_OP, 1, 5)
            counts_f = counts[:, :].bitcast(f32)
            dve.wait_ge(counts_packed, 1)
            packed = psum[0:NODES, 6, 0:GROUP]
            step(nc.vector.tensor_scalar(hi_count[:, :], packed, 1.0 / PACK, 0.375, ALU.mult, ALU.subtract))
            dve.wait_ge(dve_step, steps[0])
            step(nc.vector.tensor_scalar(counts[:, GROUP:2 * GROUP], hi_count[:, :], ROUND, ROUND,
                                         ALU.add, ALU.subtract))
            dve.wait_ge(dve_step, steps[0])
            nc.vector.scalar_tensor_tensor(counts[:, 0:GROUP], counts_f[:, GROUP:2 * GROUP], -PACK, packed,
                                           ALU.mult, ALU.add).then_inc(counts_ready, 1)
            for half, cols in enumerate(HALF_COLS):
                dve.wait_ge(x1_high_ready, half + 1)
                nc.vector.tensor_tensor(x1_low[:, cols], x1[:, cols], x1_high[:, cols].bitcast(f32),
                                        ALU.subtract).then_inc(x1_low_ready, 1)
            dve.wait_ge(degree_ready, 1)
            step(nc.vector.tensor_scalar(degree[:, :], psum[0:NODES, DEGREE_BANK, 0:2 * RELATIONS].rearrange(
                "d (r two) -> d r two", two=2)[:, :, 0], 1.0, None, ALU.max))
            dve.wait_ge(dve_step, steps[0])
            step(nc.vector.reciprocal(degree_inv[:, :], degree[:, :]))
            dve.wait_ge(dve_step, steps[0])
            nc.vector.tensor_tensor(degree_diag.rearrange("d (r n) -> d r n", r=RELATIONS),
                                    ident[0:NODES, 0:NODES].unsqueeze(1).broadcast_to([NODES, RELATIONS, NODES]),
                                    degree_inv[:, :].unsqueeze(2).broadcast_to([NODES, RELATIONS, NODES]),
                                    ALU.mult).then_inc(diag_ready, 1)
            split_low(ROOT, range(2, 4))
            dve.wait_ge(counts_ready, 1)
            dve.wait_ge(inverse_ready, 1)
            for half, bank in enumerate(INVERSE_BANKS):
                cols = slice(half * GROUP, (half + 1) * GROUP)
                last = nc.vector.tensor_tensor(adj[:, cols], psum[0:NODES, bank, 0:GROUP], counts_f[:, cols], ALU.mult)
            last.then_inc(adj_ready, 1)
            split_low(ROOT, range(4, 5))
            dve.wait_ge(adj_ready, 1)
            dve.wait_ge(adj_high_ready, 1)
            nc.vector.tensor_tensor(adj_low[:, :], adj, adj_high[:, :].bitcast(f32),
                                    ALU.subtract).then_inc(adj_low_ready, 1)
            split_low(ROOT, range(5, CHUNKS))
            step(nc.vector.tensor_scalar(twice_x1, x1[:, :], 2.0, None, ALU.mult))

            def mean_low_operand(s, relation, n):
                dve.wait_ge(mean_out, CHUNKS)
                dve.wait_ge(high_op_ready, n)
                nc.vector.tensor_tensor(low_op[s][:, :], means[:, bass.ds(relation * SPAN, SPAN)],
                                        high_op[s][:, :].bitcast(f32), ALU.subtract).then_inc(op_ready[s], 1)

            with dve.Fori(0, RELATIONS // 2) as trip:
                split_low(REL0, range(1), trip)
                mean_low_operand(0, trip * 2, trip * 2 + 6)
                split_low(REL0, range(1, CHUNKS), trip)
                split_low(REL0 + 1, range(1), trip)
                mean_low_operand(1, trip * 2 + 1, trip * 2 + 7)
                split_low(REL0 + 1, range(1, CHUNKS), trip)
            split_low(GATE_X, range(6))
            low_from_psum(0, 0, 14)
            split_low(GATE_X, range(6, 7))
            low_from_psum(0, 1, 15)
            split_low(GATE_X, range(7, CHUNKS))
            split_low(GATE_U, range(CHUNKS))
            dve.wait_ge(tanh_ready, 1)
            step(nc.vector.tensor_tensor(tanh_less_x, tanh_u, x1[:, :], ALU.subtract))
            for half, cols in enumerate(HALF_COLS):
                dve.wait_ge(dve_step, steps[0])
                dve.wait_ge(z_ready, half + 1)
                step(nc.vector.tensor_tensor(resid[:, cols], psum[0:NODES, half, :], tanh_less_x[:, cols], ALU.mult))
                dve.wait_ge(dve_step, steps[0])
                step(nc.vector.tensor_tensor(resid[:, cols], resid[:, cols], twice_x1[:, cols], ALU.add))
                dve.wait_ge(dve_step, steps[0])
                step(nc.vector.bn_stats(z_stats[:, half, :], resid[:, cols]))
            dve.wait_ge(dve_step, steps[0])
            nc.vector.bn_aggr(moments[:, 1, :], z_stats[:, :, :].rearrange("p b s -> p (b s)")).then_inc(var_ready, 1)
            dve.wait_ge(var_ready, 2)
            dve.wait_ge(std_ready, 2)
            step(nc.vector.reciprocal(rstd[:, 1:2], std[:, 1:2]))
            dve.wait_ge(dve_step, steps[0])
            nc.vector.scalar_tensor_tensor(shift[:, :], moments[:, 1, 0:1], -1.0, rstd[:, 1:2],
                                           ALU.mult, ALU.mult).then_inc(shift_ready, 1)
            nc.vector.tensor_scalar(resid[:, HALF_COLS[0]], resid[:, HALF_COLS[0]], moments[:, 1, 0:1],
                                    rstd[:, 1:2], ALU.subtract, ALU.mult).then_inc(out_ready[0], 1)

        @block.tensor
        def _(pe):
            def add(into, lhsT, rhs, start=False, stop=False):
                return nc.tensor.matmul(into, lhsT, rhs, start=start, stop=stop, skip_group_check=True)

            def product(matrix, s, acc, opened=False, ends=True, trip=None, before={}, between={}, by_half=CHUNKS):
                split = {c: (n, ring) for n, c, _, _, ring in split_chunks(matrix)}
                order = [(c, part) for c in range(by_half) for part in HALF_COLS]
                order += [(c, part) for part in HALF_COLS for c in range(by_half, CHUNKS)]
                for c, part in order:
                    into = psum[0:NODES, acc + part.start // BANK, :]
                    opens, closes = part.start == 0, part.stop == FEATURES
                    nodes = slice(c * NODES, (c + 1) * NODES)
                    first, final = c == 0 and not opened, c == CHUNKS - 1 and ends
                    if opens and c in before:
                        before[c]()
                    if c not in split:
                        slot, at = matrix % 2 * QUARTERS + c // CHUNKS_PER_QUARTER, c % CHUNKS_PER_QUARTER * FEATURES
                        if opens and matrix == K and c == 0:
                            pe.wait_ge(first_in, 16)
                        elif opens:
                            pe.wait_ge(raw_in[slot], arrivals(matrix))
                        add(into, full_op[s][:, nodes], raw[:, slot, at + part.start:at + part.stop], start=first)
                    else:
                        n, ring = split[c]
                        made = splits_before(matrix) + n + 1
                        if trip is not None:
                            made = trip * (2 * CHUNKS) + made
                        if opens:
                            pe.wait_ge(low_ready, made)
                        for lhsT, rhs in ((high_op, high), (low_op, high), (high_op, low)):
                            last = add(into, lhsT[s][:, nodes], rhs[:, ring, part],
                                       start=first and lhsT is high_op and rhs is high,
                                       stop=final and rhs is low)
                        if matrix == GATE_U and final:
                            last.then_inc(z_ready, 1)
                        elif closes:
                            last.then_inc(split_free, 1)
                    if closes and c in between:
                        between[c]()

            def transposes(bank, source, ks=range(CHUNKS)):
                for k in ks:
                    b, at = divmod(k, CHUNKS // 2)
                    last = nc.tensor.transpose(psum[:, bank + b, at * NODES:(at + 1) * NODES],
                                               source[:, k * P:(k + 1) * P], ident[0:NODES, 0:NODES])
                return last

            def transpose_product(n):
                pe.wait_ge(natural_ready, n + 1)
                if n:
                    pe.wait_ge(full_ready, n)
                else:
                    pe.wait_ge(keys_used, EDGE_CHUNKS // 4)
                transposes(TR, natural).then_inc(transposed, 1)

            def open_with_bias(acc, row):
                at = 32 * row
                for b in range(HALVES):
                    cols = slice(b * BANK, (b + 1) * BANK)
                    add(psum[0:NODES, acc + b, :], ones_r[at:at + 1, :], rows_high[at:at + 1, cols], start=True)
                    last = add(psum[0:NODES, acc + b, :], ones_r[at:at + 1, :], rows_low[at:at + 1, cols])
                last.then_inc(opened_ready, 1)

            def transpose_edges():
                pe.wait_ge(consts, CONST_IDENT)
                pe.wait_ge(edge_f_ready, 1)
                nc.tensor.transpose(psum[:, 6, 0:4 * EDGE_CHUNKS], edge_f[:, :],
                                    ident[0:4 * EDGE_CHUNKS, 0:4 * EDGE_CHUNKS]).then_inc(edges_T, 1)

            def key_differences(banks):
                pe.wait_ge(consts, CONST_KEYS)
                pe.wait_ge(pair_ready, 1)
                pe.wait_ge(edges_copied, 1)
                for bank in banks:
                    into = psum[:, KEY_BANKS[bank], :]
                    add(into, key_w[:, :], pair_b[:, bank * BANK:(bank + 1) * BANK], start=True)
                    for j in range(4):
                        edges = slice(bank * BANK + j * P, bank * BANK + (j + 1) * P)
                        add(into[:, j * P:(j + 1) * P], pair_b[:, edges], neg_key_w[:, :])
                    add(into, ident_b[:, :], not_later[:, :, :].rearrange("p c j -> p (c j)"),
                        stop=True).then_inc(keys_ready, 1)

            def cell_histories():
                pe.wait_ge(src_hot_ready, 2)
                pe.wait_ge(mask_hot_ready, EDGE_CHUNKS)
                for c in range(EDGE_CHUNKS):
                    nodes = slice(c * NODES, (c + 1) * NODES)
                    last = add(psum[0:NODES, 6, 0:NODES], src_hot[:, nodes], mask_hot[:, nodes],
                               start=c == 0, stop=c == EDGE_CHUNKS - 1)
                last.then_inc(history_ready, 1)

            def count_edges(chunks):
                pe.wait_ge(count_hot_ready, chunks[-1] + 1)
                for c in chunks:
                    last = add(psum[0:NODES, 6, 0:GROUP], src_hot[:, c * NODES:(c + 1) * NODES],
                               count_hot[:, c * GROUP:(c + 1) * GROUP], start=c == 0, stop=c == EDGE_CHUNKS - 1)
                return last

            def sum_degrees():
                pe.wait_ge(counts_ready, 1)
                for r in range(RELATIONS):
                    last = add(psum[0:NODES, DEGREE_BANK, 2 * r:2 * r + 2], counts[:, r * NODES:(r + 1) * NODES],
                               ones_r[:, 0:2], start=True, stop=True)
                last.then_inc(degree_ready, 1)

            def spread_inverses():
                pe.wait_ge(diag_ready, 1)
                for half, bank in enumerate(INVERSE_BANKS):
                    last = add(psum[0:NODES, bank, 0:GROUP], ones[0:NODES, 0:NODES],
                               degree_diag[:, half * GROUP:(half + 1) * GROUP], start=True, stop=True)
                last.then_inc(inverse_ready, 1)

            def scores(groups):
                for group in groups:
                    if SCORE_BANKS[group] == 6:
                        pe.wait_ge(history_read, 1)
                    part = slice(group % 2 * HEAD_DIM, (group % 2 + 1) * HEAD_DIM)
                    for j in range(HEADS_PER_GROUP):
                        chunk, at = group // 2 * HEADS_PER_GROUP + j, j * NODES
                        nodes = slice(chunk * NODES, (chunk + 1) * NODES)
                        last = add(psum[0:NODES, SCORE_BANKS[group], at:at + NODES], full_op[1][part, nodes],
                                   full_op[0][part, nodes], start=True, stop=True)
                    last.then_inc(scores_ready, 1)

            def transpose_probs(groups):
                for group in groups:
                    pe.wait_ge(probs_ready, group + 1)
                    for j in range(HEADS_PER_GROUP):
                        at = j * NODES
                        last = nc.tensor.transpose(psum[0:NODES, SCORE_BANKS[group], at:at + NODES],
                                                   probs[:, group * GROUP + at:group * GROUP + at + NODES],
                                                   ident[0:NODES, 0:NODES])
                    last.then_inc(probs_T_ready, 1)

            pe.wait_ge(xT_in, 16)
            product(K, X_OP, 0, before={1: lambda: pe.wait_ge(op_ready[X_OP], 1)},
                    between={2: transpose_edges, 4: lambda: key_differences(range(3)),
                             7: lambda: key_differences(range(3, 6))})
            pe.wait_ge(keys_used, 2)
            product(Q, X_OP, 2, between={2: lambda: transpose_product(K)})
            product(K2, 0, 0, before={0: lambda: pe.wait_ge(full_ready, K + 1), 1: lambda: pe.wait_ge(op_ready[0], 1)},
                    between={2: lambda: transpose_product(Q)})
            product(Q2, 1, 2, before={0: lambda: pe.wait_ge(full_ready, Q + 1), 1: lambda: pe.wait_ge(op_ready[1], 1)},
                    between={2: lambda: transpose_product(K2)})

            def first_scores():
                pe.wait_ge(full_ready, 4)
                scores([0, 1])

            product(V, X_OP, 0, between={0: cell_histories, 2: lambda: transpose_product(Q2), 4: first_scores})
            scores([2])
            for half in range(HALVES):
                if half:
                    scores([3])
                pe.wait_ge(v_natural, half + 1)
                transposes(TR, natural, range(half * CHUNKS // 2, (half + 1) * CHUNKS // 2)).then_inc(v_transposed, 1)
            product(V2, X_OP, 0,
                    before={0: lambda: pe.wait_ge(v_full, 1), 1: lambda: pe.wait_ge(op_ready[X_OP], 2),
                            4: lambda: pe.wait_ge(op_ready[X_OP], 3)},
                    between={0: lambda: transpose_probs([0]), 5: lambda: transpose_probs([1]),
                             6: lambda: transpose_probs([2])})
            transpose_probs([3])
            pe.wait_ge(probs_T_copied, 1)
            count_edges(range(4))
            pe.wait_ge(v2_ready, 1)
            pe.wait_ge(probs_T_copied, GROUPS - 1)
            pe.wait_ge(last_probs_T_copied, 1)
            by_chunk = probs_T.rearrange("m (u p k n) -> m u p k n", u=2, p=2, k=HEADS_PER_GROUP)
            for i in range(GROUPS):
                for k in range(2):
                    chunk = 2 * i + k
                    last = add(psum[:, PV_BANKS[i], k * 2 * NODES:(k + 1) * 2 * NODES],
                               v2[:, chunk * P:(chunk + 1) * P],
                               by_chunk[:, chunk // HEADS_PER_GROUP, :, chunk % HEADS_PER_GROUP, :],
                               start=True, stop=True)
                last.then_inc(pv_ready, 1)
            pe.wait_ge(rows_low_ready, 1)
            open_with_bias(0, 0)
            product(OUT, 0, 0, opened=True,
                    before={0: lambda: pe.wait_ge(attn_full, 1), 1: lambda: pe.wait_ge(op_ready[0], 2),
                            4: lambda: pe.wait_ge(op_ready[0], 3)})
            open_with_bias(U, 1)
            count_edges(range(4, 17))
            pe.wait_ge(resid_ready, HALVES)
            open_with_bias(0, 2)
            for half in range(HALVES):
                pe.wait_ge(x1_ready, half + 1)
                transposes(X1_T, x1, range(half * CHUNKS // 2, (half + 1) * CHUNKS // 2)).then_inc(transposed, 1)

            count_edges(range(17, EDGE_CHUNKS)).then_inc(counts_packed, 1)

            def sum_means(ks):
                for k in ks:
                    pe.wait_ge(x1_low_ready, 1 + k // (CHUNKS // 2))
                    pe.wait_ge(adj_low_ready, 1)
                    if k == 1:
                        pe.wait_ge(op_ready[X_OP], 5)
                    if k >= 2:
                        pe.wait_ge(mean_out, k - 1)
                    for half in range(2):
                        cols = slice(half * GROUP, (half + 1) * GROUP)
                        into = psum[:, MEAN_BANKS[k % 2] + half, 0:GROUP]
                        chunk = slice(k * P, (k + 1) * P)
                        add(into, x1_high[:, chunk], adj_high[:, cols], start=True)
                        add(into, x1_low[:, chunk], adj_high[:, cols])
                        last = add(into, x1_high[:, chunk], adj_low[:, cols], stop=True)
                    last.then_inc(mean_sum, 1)

            product(ROOT, X_OP, U, opened=True, ends=False,
                    before={0: lambda: pe.wait_ge(op_ready[X_OP], 4), 4: lambda: pe.wait_ge(op_ready[X_OP], 5)},
                    between={0: sum_degrees, 1: spread_inverses, 4: lambda: sum_means(range(CHUNKS))})
            with pe.Fori(0, RELATIONS // 2) as trip:
                pe.wait_ge(op_ready[0], trip + 4)
                product(REL0, 0, U, opened=True, trip=trip)
                pe.wait_ge(op_ready[1], trip + 2)
                product(REL0 + 1, 1, U, opened=True, trip=trip)

            def transpose_u():
                pe.wait_ge(mean_out, CHUNKS)
                pe.wait_ge(natural_ready, 5)
                transposes(X1_T, natural).then_inc(transposed, 1)

            product(GATE_X, X_OP, 0, opened=True, ends=False, between={2: transpose_u})
            product(GATE_U, 0, 0, opened=True,
                    before={0: lambda: pe.wait_ge(op_ready[0], 8), 4: lambda: pe.wait_ge(op_ready[0], 9)},
                    by_half=CHUNKS - 3)


def kernel(x, src, dst, edge_type_5, edge_type_8, L0_gnn_edge_type_weights, L0_gnn_wq, L0_gnn_bq, L0_gnn_wk,
           L0_gnn_bk, L0_gnn_wv, L0_gnn_bv, L0_gnn_wiq, L0_gnn_biq, L0_gnn_wik, L0_gnn_bik, L0_gnn_wiv,
           L0_gnn_biv, L0_gnn_wo, L0_gnn_bo, L1_gnn_weight, L1_gnn_root, L1_gnn_bias, L1_gnn_w_gate,
           L1_gnn_b_gate):
    import numpy as np
    import concourse.bacc as bacc
    from concourse import mybir as _mybir
    from concourse.bass_utils import run_bass_kernel_spmd

    def quarters(w):
        return w.reshape(QUARTERS, CHUNKS_PER_QUARTER, P, FEATURES).transpose(0, 2, 1, 3).reshape(
            QUARTERS, P, QUARTER)

    x, src, dst, type5, type8 = (np.asarray(a) for a in (x, src, dst, edge_type_5, edge_type_8))
    w_gate, relations = np.asarray(L1_gnn_w_gate), np.asarray(L1_gnn_weight)
    attention = [np.asarray(w).T for w in (L0_gnn_wk, L0_gnn_wq, L0_gnn_wik, L0_gnn_wiq, L0_gnn_wv, L0_gnn_wiv,
                                           L0_gnn_wo)]
    stream = attention + [np.asarray(L1_gnn_root)] + list(relations) + [w_gate[FEATURES:], w_gate[:FEATURES]]
    biases = [np.asarray(b).reshape(CHUNKS, P).T for b in (L0_gnn_bk, L0_gnn_bq, L0_gnn_bik, L0_gnn_biq,
                                                           L0_gnn_bv, L0_gnn_biv)]
    arrays = {
        "weights": np.concatenate([quarters(w) for w in stream]),
        "xT": x.reshape(NODES, CHUNKS, P).transpose(2, 1, 0).reshape(P, SPAN),
        "x": x,
        "edge_rows": np.concatenate([a.reshape(EDGE_CHUNKS, P) for a in (src, dst, type5, type8)]),
        "edge_pair": np.stack([src, dst]),
        "type_weights": np.broadcast_to(np.asarray(L0_gnn_edge_type_weights), (NODES, CLASSES)),
        "bias_T": np.stack(biases, axis=1),
        "bias_rows": np.stack([np.asarray(b) for b in (L0_gnn_bo, L1_gnn_bias, L1_gnn_b_gate)]),
    }
    nc = bacc.Bacc("TRN2", target_bir_lowering=False, num_devices=1)
    given, args = {}, []
    for name, a in arrays.items():
        given[f"in_{name}"] = np.ascontiguousarray(a)
        args.append(nc.dram_tensor(f"in_{name}", a.shape, _mybir.dt.from_np(a.dtype), kind="ExternalInput").ap())
    out = nc.dram_tensor("out", (NODES, FEATURES), _mybir.dt.float32, kind="ExternalOutput").ap()
    gnn_block(nc, *args, out)
    r = run_bass_kernel_spmd(nc, [given], core_ids=[0])
    return r.results[0]["out"]
```
